# Optimizing a Trainium2 kernel written in Bass

```python
import numpy as np
import jax
import jax.numpy as jnp

def _softmax(x, axis=-1):
    return jax.nn.softmax(x, axis=axis)

def _gelu(x):
    return jax.nn.gelu(x, approximate=True)

def _silu(x):
    return jax.nn.silu(x)

def _sigmoid(x):
    return jax.nn.sigmoid(x)

def _layernorm(x, axis=-1, eps=1e-05):
    m = jnp.mean(x, axis=axis, keepdims=True)
    v = jnp.var(x, axis=axis, keepdims=True)
    return (x - m) / jnp.sqrt(v + eps)

def _scatter_add(tgt, idx, src, axis=0):
    return tgt.at[idx].add(src)

def _segment_sum(src, seg, n):
    return jax.ops.segment_sum(src, seg, n)
kernel_name = 'mk_seq_preln_d1_jaxref_r4_b5dd26'

def setup_inputs(seed: int=0):
    np.random.seed(seed)
    _w = jnp.asarray

    def _L0_attn_setup():
        import jax, jax.numpy as jnp
        import numpy as np
        B_SZ, L, D, N = (2, 512, 256, 16)
        key = jax.random.key(seed)
        ks = jax.random.split(key, 8)
        x = jax.random.normal(ks[0], (B_SZ, L, D), dtype=jnp.float32)
        s1 = 1.0 / np.sqrt(D)
        W1 = jax.random.uniform(ks[1], (D, D), minval=-s1, maxval=s1, dtype=jnp.float32)
        b1 = jax.random.uniform(ks[2], (D,), minval=-s1, maxval=s1, dtype=jnp.float32)
        W2 = jax.random.uniform(ks[3], (N, D), minval=-s1, maxval=s1, dtype=jnp.float32)
        b2 = jax.random.uniform(ks[4], (N,), minval=-s1, maxval=s1, dtype=jnp.float32)
        W3 = jax.random.uniform(ks[5], (N, D), minval=-s1, maxval=s1, dtype=jnp.float32)
        b3 = jax.random.uniform(ks[6], (N,), minval=-s1, maxval=s1, dtype=jnp.float32)
        lim = np.sqrt(6.0 / (D + N))
        A = jax.random.uniform(ks[7], (D, N), minval=-lim, maxval=lim, dtype=jnp.float32)
        return {'x': x, 'W1': W1, 'b1': b1, 'W2': W2, 'b2': b2, 'W3': W3, 'b3': b3, 'A': A}
    _L0_attn_in = _L0_attn_setup()

    def _L0_ffn_setup():
        import jax, jax.numpy as jnp
        import numpy as np
        TOP_K = 2
        key = jax.random.key(seed)
        k1, k2, k3, k4, k5 = jax.random.split(key, 5)
        B, S, D, F, E = (2, 256, 256, 512, 8)
        return {'x': jax.random.normal(k1, (B, S, D), dtype=jnp.float32), 'router_kernel_DE': jax.random.normal(k2, (D, E), dtype=jnp.float32) * 0.02, 'kernel_gating_EDF': jax.random.normal(k3, (E, D, F), dtype=jnp.float32) * 0.02, 'kernel_up_EDF': jax.random.normal(k4, (E, D, F), dtype=jnp.float32) * 0.02, 'kernel_down_EFD': jax.random.normal(k5, (E, F, D), dtype=jnp.float32) * 0.02}
    _L0_ffn_in = _L0_ffn_setup()
    _d = {'L0_attn_x': _L0_attn_in['x'], 'L0_attn_W1': _L0_attn_in['W1'], 'L0_attn_b1': _L0_attn_in['b1'], 'L0_attn_W2': _L0_attn_in['W2'], 'L0_attn_b2': _L0_attn_in['b2'], 'L0_attn_W3': _L0_attn_in['W3'], 'L0_attn_b3': _L0_attn_in['b3'], 'L0_attn_A': _L0_attn_in['A'], 'L0_ffn_router_kernel_DE': _L0_ffn_in['router_kernel_DE'], 'L0_ffn_kernel_gating_EDF': _L0_ffn_in['kernel_gating_EDF'], 'L0_ffn_kernel_up_EDF': _L0_ffn_in['kernel_up_EDF'], 'L0_ffn_kernel_down_EFD': _L0_ffn_in['kernel_down_EFD']}
    _x0 = _d['L0_attn_x']
    _d['L0_attn_x'] = jax.random.normal(jax.random.fold_in(jax.random.key(seed), 1), (8, 1024, 256), dtype=_x0.dtype)
    del _x0
    return _d

def reference(L0_attn_x, L0_attn_W1, L0_attn_b1, L0_attn_W2, L0_attn_b2, L0_attn_W3, L0_attn_b3, L0_attn_A, L0_ffn_router_kernel_DE, L0_ffn_kernel_gating_EDF, L0_ffn_kernel_up_EDF, L0_ffn_kernel_down_EFD):

    def _L0_attn_ref(x, W1, b1, W2, b2, W3, b3, A):
        import jax, jax.numpy as jnp
        import numpy as np
        B_SZ, L, D, N = (2, 512, 256, 16)
        delta = jax.nn.softplus(x @ W1.T + b1)
        Bm = x @ W2.T + b2
        Cm = x @ W3.T + b3
        dB = jnp.einsum('bld,bln->bldn', delta, Bm)
        h = x[..., None] * dB
        y = jnp.einsum('bln,bldn->bld', Cm, h)
        return y

    def _L0_ffn_ref(x, router_kernel_DE, kernel_gating_EDF, kernel_up_EDF, kernel_down_EFD):
        import jax, jax.numpy as jnp
        import numpy as np
        TOP_K = 2
        E = router_kernel_DE.shape[-1]
        x = x.astype(jnp.float32)
        logits_BSE = jnp.einsum('BSD,DE->BSE', x, router_kernel_DE)
        probs_BSE = jax.nn.softmax(logits_BSE.astype(jnp.float32), axis=-1)
        weights_BSK, indices_BSK = jax.lax.top_k(probs_BSE, TOP_K)
        norm_weights_BSK = jax.nn.softmax(weights_BSK, axis=-1)
        one_hot_BSKE = jax.nn.one_hot(indices_BSK, num_classes=E, dtype=x.dtype)
        full_weights_BSE = jnp.sum(one_hot_BSKE * norm_weights_BSK[..., None], axis=2)
        gating_BSEF = jnp.einsum('BSD,EDF->BSEF', x, kernel_gating_EDF)
        act_BSEF = jax.nn.silu(gating_BSEF)
        up_BSEF = jnp.einsum('BSD,EDF->BSEF', x, kernel_up_EDF)
        fuse_BSEF = act_BSEF * up_BSEF
        down_BSED = jnp.einsum('BSEF,EFD->BSED', fuse_BSEF, kernel_down_EFD)
        out_BSD = jnp.einsum('BSED,BSE->BSD', down_BSED, full_weights_BSE)
        return out_BSD.astype(jnp.float32)
    x = L0_attn_x
    x = x + _L0_attn_ref(_layernorm(x, axis=-1), L0_attn_W1, L0_attn_b1, L0_attn_W2, L0_attn_b2, L0_attn_W3, L0_attn_b3, L0_attn_A)
    x = x + _L0_ffn_ref(_layernorm(x, axis=-1), L0_ffn_router_kernel_DE, L0_ffn_kernel_gating_EDF, L0_ffn_kernel_up_EDF, L0_ffn_kernel_down_EFD)
    return x

_drawn_inputs = setup_inputs


def setup_inputs(seed=0):
    import zlib

    import numpy as np

    out = dict(_drawn_inputs(seed))
    spreads = {}
    factors = {'L0_attn_b1': 2.943,
     'L0_ffn_router_kernel_DE': 5.341,
     'L0_ffn_kernel_gating_EDF': 4.648,
     'L0_ffn_kernel_up_EDF': 4.603,
     'L0_ffn_kernel_down_EFD': 4.607}
    for name, (base, spread) in spreads.items():
        noise = np.random.default_rng([zlib.crc32(name.encode()), seed]).standard_normal(out[name].shape)
        drawn = base * np.exp(spread * noise) if base else spread * noise
        out[name] = jnp.asarray(drawn.astype(out[name].dtype))
    for name, factor in factors.items():
        out[name] = (out[name] * factor).astype(out[name].dtype)
    return out
```

```python
import concourse.bass as bass
from concourse import mybir
from contextlib import ExitStack

P = 128
D = 256
DC = D // P
TOKENS = 8 * 1024
COLS = TOKENS // P
G = 4
GROUPS = COLS // G
N = 16
NZ = D + 2 * N
E = 8
F = 512
FC = F // P
EXPERT = 2 * DC * F + FC * D
QUARTERS = 4
Q = EXPERT // QUARTERS
TOP_K = 2
EPS = 1e-5

REGION = TOKENS + P
ID = D
WT = D + 1
ROW = D + 1 + E
TILES = -(-(TOP_K * TOKENS // P + E - 1) // 4) * 4
DUMMY = E * REGION
DUMP = TOKENS

EARLY = 6
LOOP_FROM, LOOP_TO = 4, GROUPS
SLOTS = GROUPS + 2
LINKS = 35


def moe_program(nc, x_in, wz_in, bz_in, router_in, experts_in, out):
    f32, f32r, bf16 = mybir.dt.float32, mybir.dt.float32r, mybir.dt.bfloat16
    i32, u32 = mybir.dt.int32, mybir.dt.uint32
    ALU = mybir.AluOpType
    ACT = mybir.ActivationFunctionType
    X = mybir.AxisListType.X

    sorted_rows = nc.dram_tensor("sorted_rows", (DUMMY + P, ROW), f32, kind="Internal").ap()
    x_cols = x_in.rearrange("(p t) d -> p t d", t=COLS)
    out_cols = out[0:TOKENS, :].rearrange("(p t) d -> p t d", t=COLS)

    at = [-(-nc.sbuf_base // 32) * 32]

    def place(name, shape, dt):
        size = 1
        for s in shape[1:]:
            size *= s
        size *= 2 if dt == bf16 else 4
        t = nc.alloc_sbuf_tensor_at(name, shape, dt, offset=at[0])
        at[0] += -(-size // 32) * 32
        return t

    ident = place("ident", [P, P], f32)
    table = place("table", [1, 2, TILES], i32)
    weights_at = at[0]
    wall = place("wall", [P, 2 * E, EXPERT], f32r)
    moe_at = at[0]

    at[0] = weights_at + 2 * EARLY * EXPERT * 4
    x = place("x", [P, 4, G, D], f32)
    xn = place("xn", [P, 2, G, D], f32)
    xt_hi = place("xt_hi", [P, G, DC, P], f32r)
    xt_lo = place("xt_lo", [P, G, DC, P], f32r)
    sp = place("sp", [P, G, D], f32)
    rows = place("rows", [P, 2, G, ROW], f32)
    xt2 = place("xt2", [P, G // 2, DC, P], f32)
    wz = place("wz", [P, 2, DC, NZ], f32r)
    bz = place("bz", [2, NZ], f32r)
    ones_row = place("ones_row", [2, P], f32r)
    stage = place("stage", [P, 2, Q], f32)
    router = place("router", [P, DC, E], f32)
    upper = place("upper", [P, P], bf16)
    ones = place("ones", [P, P], bf16)
    ids = place("ids", [P, COLS], i32)
    prio = place("prio", [P, E], f32)
    region = place("region", [P, E], f32)
    pidx = place("pidx", [P, 1], f32)
    base = place("base", [P, E], f32)
    stats_x = place("stats_x", [P, G, 6], f32)
    stats_x2 = place("stats_x2", [P, G, 6], f32)
    mv1 = place("mv1", [P, G, 2], f32)
    mv2 = place("mv2", [P, G, 2], f32)
    ln1 = place("ln1", [P, G], f32)
    y1 = place("y1", [P, G], f32)
    ln2 = place("ln2", [P, G], f32)
    y2 = place("y2", [P, G], f32)
    nw = place("nw", [P, 3, G], f32)
    rstd = place("rstd", [P, 2, G], f32)
    cc = place("cc", [P, G, N], f32)
    bc = place("bc", [P, G, N], f32)
    s_bc = place("s_bc", [P, G], f32)
    g4 = place("g4", [P, 10, G], f32)
    g32 = place("g32", [P, 7, G, E], f32)
    chosen = place("chosen", [P, G, E], bf16)
    pos = place("pos", [P, 2, TOP_K, G], u32)
    pads = place("pads", [P, E], u32)
    assert at[0] <= nc.sbuf_usable_end, (at[0], nc.sbuf_usable_end)

    wz_raw = x[:, 3].rearrange("p a b -> p (a b)")[:, 0:DC * NZ]
    bz_raw = sp[0:1, 0:2].rearrange("p a b -> p (a b)")[:, 0:NZ]
    bz_low = sp[0:1, 2:4].rearrange("p a b -> p (a b)")[:, 0:NZ]

    at[0] = moe_at
    stage2_at = at[0]
    xg_t = place("xg_t", [P, 2, 2, DC, P], f32r)
    h = place("h", [P, F], f32)
    ht = place("ht", [P, 2, FC, P], f32r)
    y = place("y", [P, 2, D], f32)
    xg = place("xg", [P, 2, ROW], f32)
    idw = place("idw", [P, 4, 1 + E], i32)
    assert at[0] <= nc.sbuf_usable_end, (at[0], nc.sbuf_usable_end)
    at[0] = stage2_at
    stage2 = place("stage2", [P, 2, Q], f32)

    ctx = ExitStack()
    with ctx:
        def sem(name):
            return ctx.enter_context(nc.semaphore(name))

        z = ctx.enter_context(nc.psum_tensor("z", [P, G, 512], f32))
        psum = [z[:, i] for i in range(G)] + [
            ctx.enter_context(nc.psum_tensor(f"bank{i}", [P, 512], f32))[:] for i in range(G, 8)]
        z_view = z[:, :, 0:NZ]

        consts = sem("consts")
        ident0 = sem("ident0")
        wz_loaded = sem("wz_loaded")
        wz_hi = sem("wz_hi")
        bz_in_place = sem("bz_in_place")
        wz_lo = sem("wz_lo")
        x_loaded = [sem(f"x_loaded{i}") for i in range(4)]
        x2_stored = [sem(f"x2_stored{i}") for i in range(4)]
        stats1 = sem("stats1")
        rs1 = sem("rs1")
        xn1 = sem("xn1")
        t1_done = sem("t1_done")
        hi1 = sem("hi1")
        lo1 = sem("lo1")
        z_done = sem("z_done")
        z_free = sem("z_free")
        soft = sem("soft")
        y_done = sem("y_done")
        x2_done = sem("x2_done")
        stats2 = sem("stats2")
        rs2 = sem("rs2")
        xn2 = sem("xn2")
        t2_done = sem("t2_done")
        xt2_done = sem("xt2_done")
        logits = sem("logits")
        shifted = sem("shifted")
        exps = sem("exps")
        gap = sem("gap")
        gap_exp = sem("gap_exp")
        chose = sem("chose")
        ranks = sem("ranks")
        placed = sem("placed")
        ids_in = sem("ids_in")
        scattered = [sem(f"scattered{i}") for i in range(2)]
        stage_in = [sem(f"stage_in{i}") for i in range(2)]
        w_hi = sem("w_hi")
        w_lo = sem("w_lo")
        act_own = sem("act_own")
        dve_own = sem("dve_own")
        passed = {nc.gpsimd: sem("pool_passed"), nc.vector: sem("dve_passed")}
        pad_row = sem("pad_row")
        pad_at = sem("pad_at")
        padded = sem("padded")
        tabled = sem("tabled")

        flat = x[0:1, 0:3].rearrange("p a g d -> p (a g d)")
        tile_no = flat[:, 0:TILES]

        class Own:

            def __init__(self, eng, semaphore):
                self.eng, self.sem, self.base, self.n = eng, semaphore, 0, 0

            def mark(self, instruction):
                instruction.then_inc(self.sem, 1)
                self.n += 1

            def wait(self):
                self.eng.wait_ge(self.sem, self.base + self.n)

        def run_slots(eng, slot, own=None, per_slot=0):
            for g in range(LOOP_FROM):
                slot(g, g % 4, g // 4, g)
            if own:
                start = own.base + own.n
            with eng.Fori(0, (LOOP_TO - LOOP_FROM) // 4) as j:
                if own:
                    own.base, own.n = start + j * (4 * per_slot), 0
                for u in range(LOOP_FROM, LOOP_FROM + 4):
                    slot(4 * j + u, u % 4, j + u // 4, u, j)
                if own:
                    assert own.n == 4 * per_slot, own.n
            if own:
                own.base, own.n = start + per_slot * (LOOP_TO - LOOP_FROM), 0
            for g in range(LOOP_TO, SLOTS):
                slot(g, g % 4, g // 4, g)

        def parts(u, j):
            return (u < GROUPS, 1 <= u <= GROUPS, 2 <= u, j is not None)

        def need(eng, semaphore, value):
            if not isinstance(value, int) or value > 0:
                eng.wait_ge(semaphore, value)

        def wait_apart(eng, semaphore, value):
            eng.wait_ge(semaphore, value)
            eng.sem_inc(passed[eng], 1)

        def before(b, r, n):
            return (b - n) % 4, r - (1 if b < n else 0)

        def quarter(u, j, i):
            k = 2 * (u - LOOP_FROM) + i
            return 2 * j + k // QUARTERS, k % QUARTERS

        with nc.Block() as block:

            @block.sync
            def _(eng):
                def load_x(g, b):
                    eng.dma_start(x[:, b], x_cols[:, bass.ds(g * G, G), :]).then_inc(x_loaded[b], 16)

                def store_x2(g, b):
                    eng.wait_ge(x2_done, g + 1)
                    eng.dma_start(out_cols[:, bass.ds(g * G, G), :], x[:, b]).then_inc(x2_stored[b], 16)

                load_x(0, 0)
                eng.dma_start(wz_raw, wz_in).then_inc(wz_loaded, 16)
                eng.dma_start(bz_raw, bz_in).then_inc(wz_loaded, 16)
                eng.dma_start(router[:], router_in).then_inc(wz_loaded, 16)
                load_x(1, 1)
                load_x(2, 2)
                eng.wait_ge(wz_lo, 4)
                eng.dma_start(bz[1:2, :].bitcast(f32), bz_low).then_inc(bz_in_place, 16)
                load_x(3, 3)
                with eng.Fori(0, GROUPS // 4 - 1) as j:
                    for u in range(4):
                        g = 4 * j + 4 + u
                        store_x2(4 * j + u, u)
                        eng.wait_ge(xn2, 4 * G * j + G * (u + 1))
                        eng.wait_ge(x2_stored[u], 16 * (j + 1))
                        eng.wait_ge(wz_loaded, 48)
                        load_x(g, u)
                        for i in range(2):
                            k = 8 * j + 2 * u + i
                            eng.wait_ge(w_lo, k + 1)
                            eng.dma_start(stage[:, i], experts_in[bass.ds(k, 1), :, :]
                                          .rearrange("a p n -> p (a n)")).then_inc(stage_in[i], 16)
                for b in range(4):
                    store_x2(GROUPS - 4 + b, b)
                for b in range(4):
                    eng.wait_ge(x2_stored[b], GROUPS // 4 * 16)

            @block.gpsimd
            def _(eng):
                eng.memset(ident[:], 0.0).then_inc(ident0, 1)
                eng.memset(upper[:], 0.0).then_inc(ident0, 1)
                eng.memset(ones[:], 1.0).then_inc(consts, 1)
                eng.iota(ids[:], pattern=[[1, COLS]], base=0, channel_multiplier=COLS).then_inc(consts, 1)
                eng.iota(prio[:], pattern=[[-1, E]], base=E, channel_multiplier=0,
                         allow_small_or_imprecise_dtypes=True).then_inc(consts, 1)
                eng.iota(region[:], pattern=[[REGION, E]], base=0, channel_multiplier=0,
                         allow_small_or_imprecise_dtypes=True).then_inc(consts, 1)
                eng.iota(pidx[:], pattern=[[0, 1]], base=0, channel_multiplier=1,
                         allow_small_or_imprecise_dtypes=True).then_inc(consts, 1)
                eng.wait_ge(consts, 5)
                eng.wait_ge(ident0, 2)
                eng.affine_select(out=ident[:], in_=ident[:], compare_op=ALU.not_equal, fill=1.0, base=0,
                                  pattern=[[-1, P]], channel_multiplier=1).then_inc(consts, 1)
                eng.affine_select(out=upper[:], in_=upper[:], compare_op=ALU.is_ge, fill=1.0, base=0,
                                  pattern=[[-1, P]], channel_multiplier=1).then_inc(consts, 1)

                def slot(g, b, r, u, j=None):
                    first, second, third, weights = parts(u, j)
                    if second:
                        b1, r1 = before(b, r, 1)
                        eng.wait_ge(y_done, g)
                        eng.tensor_tensor(x[:, b1], x[:, b1], sp[:], ALU.add).then_inc(x2_done, 1)
                        b3, r3 = before(b, r, 3)
                        if u >= 3:
                            wait_apart(eng, scattered[(u - 3) % 2], 128 * (2 * r3 + b3 // 2 + 1))
                        eng.tensor_copy(rows[:, (u - 1) % 2, :, ID].bitcast(i32),
                                        ids[:, bass.ds((g - 1) * G, G)]).then_inc(ids_in, 1)
                    if third:
                        b2, r2 = before(b, r, 2)
                        eng.wait_ge(placed, g - 1)
                        wait_apart(eng, ids_in, g - 1)
                        for k in range(TOP_K):
                            for c in range(G):
                                eng.indirect_dma_start(
                                    sorted_rows, bass.IndirectOffsetOnAxis(pos[:, u % 2, k, c:c + 1], 0),
                                    rows[:, u % 2, c, :], None).then_inc(scattered[u % 2], 16)

                run_slots(eng, slot)
                for b in range(4):
                    eng.wait_ge(x2_stored[b], GROUPS // 4 * 16)
                eng.iota(tile_no, pattern=[[1, TILES]], base=0, channel_multiplier=0,
                         allow_small_or_imprecise_dtypes=True).then_inc(tabled, 1)
                for i in range(2):
                    eng.wait_ge(scattered[i], GROUPS // 2 * TOP_K * G * 16)
                pad = rows[:, 0, 0, :]
                eng.memset(pad, 0.0).then_inc(pad_row, 1)
                eng.wait_ge(pad_row, 1)
                eng.iota(pad[:, ID:ID + 1].bitcast(i32), pattern=[[0, 1]], base=DUMP,
                         channel_multiplier=1).then_inc(pad_row, 1)
                eng.wait_ge(pad_row, 2)
                eng.wait_ge(pad_at, 1)
                for e in range(E):
                    eng.indirect_dma_start(sorted_rows, bass.IndirectOffsetOnAxis(pads[:, e:e + 1], 0),
                                           pad, None).then_inc(padded, 16)
                eng.dma_start(sorted_rows[DUMMY:DUMMY + P, :], pad).then_inc(padded, 16)
                eng.dma_start(out[DUMP:DUMP + P, :], pad[:, 0:D]).then_inc(padded, 16)
                eng.wait_ge(padded, (E + 2) * 16)

            @block.scalar
            def _(eng):
                own = Own(eng, act_own)
                nc.scalar.preload_act_table_set("natural_log_exp_and_others")
                eng.wait_ge(wz_loaded, 48)
                nc.scalar.activation(wz[:, 0].rearrange("p c n -> p (c n)"), wz_raw, ACT.Copy).then_inc(wz_hi, 1)
                nc.scalar.activation(bz[0:1, :], bz_raw, ACT.Copy).then_inc(wz_hi, 1)
                eng.wait_ge(wz_lo, 4)
                eng.wait_ge(bz_in_place, 16)

                def slot(g, b, r, u, j=None):
                    first, second, third, weights = parts(u, j)
                    if third:
                        eng.wait_ge(shifted, g - 1)
                        nc.scalar.activation(g32[:, 1], g32[:, 0], ACT.Exp).then_inc(exps, 1)
                        eng.wait_ge(gap, g - 1)
                        nc.scalar.activation(g4[:, 6], g4[:, 5], ACT.Exp).then_inc(gap_exp, 1)
                    if first:
                        eng.wait_ge(stats1, g + 1)
                        own.mark(nc.scalar.activation(ln1[:], mv1[:, :, 1], ACT.Ln, bias=EPS))
                        own.wait()
                        nc.scalar.activation(y1[:], ln1[:], ACT.Exp, scale=-0.5).then_inc(rs1, 1)
                    if second:
                        eng.wait_ge(stats2, g)
                        own.mark(nc.scalar.activation(ln2[:], mv2[:, :, 1], ACT.Ln, bias=EPS))
                        own.wait()
                        nc.scalar.activation(y2[:], ln2[:], ACT.Exp, scale=-0.5).then_inc(rs2, 1)
                    if first:
                        need(eng, z_done, g)
                        for half in range(2):
                            eng.wait_ge(t1_done, 2 * g + half + 1)
                            nc.scalar.activation(xt_hi[:, 2 * half:2 * half + 2].rearrange("p a c n -> p (a c n)"),
                                                 psum[4 + half], ACT.Copy).then_inc(hi1, 1)
                    if second:
                        for half in range(2):
                            eng.wait_ge(t2_done, 2 * g - 1 + half)
                            need(eng, logits, 2 * (g - 1) + half)
                            nc.scalar.activation(xt2[:].rearrange("p a c n -> p (a c n)"),
                                                 psum[6], ACT.Copy).then_inc(xt2_done, 1)
                    if weights:
                        for i in range(2):
                            e, q = quarter(u, j, i)
                            k = 2 * (g - LOOP_FROM) + i
                            eng.wait_ge(stage_in[i], (g - LOOP_FROM + 1) * 16)
                            nc.scalar.activation(wall[:, bass.ds(2 * e, 1), q * Q:(q + 1) * Q]
                                                 .rearrange("p a n -> p (a n)"), stage[:, i], ACT.Copy).then_inc(w_hi, 1)
                    if first:
                        eng.wait_ge(z_done, g + 1)
                        need(eng, x2_done, g)
                        nc.scalar.activation(cc[:], z_view[:, :, D + N:NZ], ACT.Copy)
                        own.mark(nc.scalar.activation(sp[:], z_view[:, :, 0:D], ACT.Abs))
                        own.wait()
                        own.mark(nc.scalar.activation(sp[:], sp[:], ACT.Exp, scale=-1.0))
                        own.wait()
                        nc.scalar.activation(sp[:], sp[:], ACT.Ln, bias=1.0).then_inc(soft, 1)

                run_slots(eng, slot, own, 4)

            @block.vector
            def _(eng):
                own = Own(eng, dve_own)
                V = nc.vector
                V.memset(stage[0:2, 0, 0:P], 1.0).then_inc(wz_lo, 1)
                eng.wait_ge(consts, 7)
                eng.wait_ge(wz_lo, 1)
                V.tensor_copy(ones_row[:], stage[0:2, 0, 0:P]).then_inc(wz_lo, 1)
                V.tensor_copy(base[:], region[:]).then_inc(dve_own, 1)
                own.n = 1
                eng.wait_ge(wz_hi, 2)
                V.tensor_tensor(bz_low, bz_raw, bz[0:1, :].bitcast(f32), ALU.subtract).then_inc(wz_lo, 1)
                V.tensor_tensor(wz[:, 1].rearrange("p c n -> p (c n)"), wz_raw,
                                wz[:, 0].rearrange("p c n -> p (c n)").bitcast(f32), ALU.subtract).then_inc(wz_lo, 1)

                def bcast(a):
                    return a.unsqueeze(2).to_broadcast([P, G, E])

                def measure(src, stats, mv, done):
                    for c in range(G):
                        last = V.bn_stats(stats[:, c], src[:, c])
                    own.mark(last)
                    wait_apart(eng, own.sem, own.base + own.n)
                    for c in range(G):
                        last = V.bn_aggr(mv[:, c], stats[:, c])
                    last.then_inc(done, 1)

                def newton(mv, y0, res):
                    own.mark(V.tensor_tensor(nw[:, 0], y0[:], y0[:], ALU.mult))
                    own.wait()
                    own.mark(V.scalar_tensor_tensor(nw[:, 1], mv[:, :, 1], EPS, nw[:, 0], ALU.add, ALU.mult))
                    own.wait()
                    own.mark(V.tensor_scalar(nw[:, 2], nw[:, 1], -0.5, 1.5, ALU.mult, ALU.add))
                    own.wait()
                    own.mark(V.tensor_tensor(res, y0[:], nw[:, 2], ALU.mult))
                    own.wait()

                mx, rec, m1, best1, best2, dlt, edl, w1, w2, tmp4 = (g4[:, i] for i in range(10))
                lsh, ex, pr, t32, oh1, oh2, u32_ = (g32[:, i] for i in range(7))
                lg = psum[7][:, 0:G * E].rearrange("p (g e) -> p g e", g=G)
                rank = psum[7][:, 64:64 + G * E].rearrange("p (g e) -> p g e", g=G)
                total = psum[7][:, 128:128 + E]

                def first_of(values, top, hot, best):
                    own.mark(V.tensor_tensor(t32, values, bcast(top), ALU.is_equal))
                    own.wait()
                    own.mark(V.tensor_tensor(t32, t32, prio[:].unsqueeze(1).to_broadcast([P, G, E]), ALU.mult))
                    own.wait()
                    own.mark(V.tensor_reduce(best, t32, X, ALU.max))
                    own.wait()
                    own.mark(V.tensor_tensor(hot, t32, bcast(best), ALU.is_equal))
                    own.wait()

                def slot(g, b, r, u, j=None):
                    first, second, third, weights = parts(u, j)
                    b1, r1 = before(b, r, 1)
                    if third:
                        eng.wait_ge(logits, 2 * (g - 1))
                        own.mark(V.tensor_reduce(mx, lg, X, ALU.max))
                        own.wait()
                        V.tensor_tensor(lsh, lg, bcast(mx), ALU.subtract).then_inc(shifted, 1)
                    if second:
                        eng.wait_ge(soft, g)
                        own.mark(V.tensor_tensor(bc[:], z_view[:, :, D:D + N], cc[:], ALU.mult))
                        V.scalar_tensor_tensor(sp[:], z_view[:, :, 0:D], 0.0, sp[:], ALU.max, ALU.add)\
                            .then_inc(z_free, 1)
                        own.wait()
                        own.mark(V.tensor_reduce(s_bc[:], bc[:], X, ALU.add))
                        own.wait()
                        eng.wait_ge(z_free, g)
                        for c in range(G):
                            last = V.scalar_tensor_tensor(sp[:, c], xn[:, (u - 1) % 2, c], s_bc[:, c:c + 1],
                                                          sp[:, c], ALU.mult, ALU.mult)
                        last.then_inc(y_done, 1)
                    if third:
                        eng.wait_ge(exps, g - 1)
                        own.mark(V.tensor_reduce(tmp4, ex, X, ALU.add))
                        own.wait()
                        own.mark(V.reciprocal(rec, tmp4))
                        own.wait()
                        own.mark(V.tensor_tensor(pr, ex, bcast(rec), ALU.mult))
                        own.wait()
                        own.mark(V.tensor_reduce(m1, pr, X, ALU.max))
                        own.wait()
                        first_of(pr, m1, oh1, best1)
                        own.mark(V.scalar_tensor_tensor(pr, oh1, -2.0, pr, ALU.mult, ALU.add))
                        own.wait()
                        own.mark(V.tensor_reduce(tmp4, pr, X, ALU.max))
                        own.wait()
                        V.tensor_tensor(dlt, tmp4, m1, ALU.subtract).then_inc(gap, 1)
                        first_of(pr, tmp4, oh2, best2)
                        V.tensor_tensor(chosen[:], oh1, oh2, ALU.add).then_inc(chose, 1)
                    if first:
                        eng.wait_ge(x_loaded[b], (r + 1) * 16)
                        measure(x[:, b], stats_x, mv1, stats1)
                    if second:
                        eng.wait_ge(x2_done, g)
                        measure(x[:, b1], stats_x2, mv2, stats2)
                    if third:
                        eng.wait_ge(gap_exp, g - 1)
                        own.mark(V.tensor_scalar(tmp4, edl, 1.0, None, ALU.add))
                        own.wait()
                        own.mark(V.reciprocal(w1, tmp4))
                        own.wait()
                        own.mark(V.tensor_tensor(w2, edl, w1, ALU.mult))
                        own.mark(V.tensor_tensor(t32, oh1, bcast(w1), ALU.mult))
                        own.wait()
                        own.mark(V.tensor_tensor(pr, oh2, bcast(w2), ALU.mult))
                        own.wait()
                        V.tensor_tensor(rows[:, u % 2, :, WT:WT + E], t32, pr, ALU.add)
                        eng.wait_ge(ranks, g - 1)
                        own.mark(V.tensor_tensor(u32_, rank, base[:].unsqueeze(1).to_broadcast([P, G, E]), ALU.add))
                        own.wait()
                        own.mark(V.tensor_tensor(t32, oh1, u32_, ALU.mult))
                        own.mark(V.tensor_tensor(pr, oh2, u32_, ALU.mult))
                        own.wait()
                        with nc.allow_low_precision(reason="row numbers, exact in float32"):
                            V.tensor_reduce(pos[:, u % 2, 0], t32, X, ALU.add)
                            V.tensor_reduce(pos[:, u % 2, 1], pr, X, ALU.add)
                        V.tensor_tensor(base[:], base[:], total, ALU.add).then_inc(placed, 1)
                    if first:
                        eng.wait_ge(rs1, g + 1)
                        newton(mv1, y1, rstd[:, 0])
                        for c in range(G):
                            V.tensor_scalar(xn[:, u % 2, c], x[:, b, c], mv1[:, c, 0:1], rstd[:, 0, c:c + 1],
                                            ALU.subtract, ALU.mult).then_inc(xn1, 1)
                    if second:
                        eng.wait_ge(rs2, g)
                        newton(mv2, y2, rstd[:, 1])
                        if u >= 3:
                            b3, r3 = before(b, r, 3)
                            eng.wait_ge(scattered[(u - 3) % 2], 128 * (2 * r3 + b3 // 2 + 1))
                        for c in range(G):
                            V.tensor_scalar(rows[:, (u - 1) % 2, c, 0:D], x[:, b1, c], mv2[:, c, 0:1],
                                            rstd[:, 1, c:c + 1], ALU.subtract, ALU.mult).then_inc(xn2, 1)
                    if first:
                        for half in range(2):
                            eng.wait_ge(hi1, 2 * g + half + 1)
                            V.tensor_tensor(xt_lo[:, 2 * half:2 * half + 2].rearrange("p a c n -> p (a c n)"),
                                            psum[4 + half],
                                            xt_hi[:, 2 * half:2 * half + 2].rearrange("p a c n -> p (a c n)")
                                            .bitcast(f32), ALU.subtract).then_inc(lo1, 1)
                    if weights:
                        for i in range(2):
                            e, q = quarter(u, j, i)
                            k = 2 * (g - LOOP_FROM) + i
                            eng.wait_ge(w_hi, k + 1)
                            V.tensor_tensor(
                                wall[:, bass.ds(2 * e + 1, 1), q * Q:(q + 1) * Q].rearrange("p a n -> p (a n)"),
                                stage[:, i],
                                wall[:, bass.ds(2 * e, 1), q * Q:(q + 1) * Q].rearrange("p a n -> p (a n)")
                                .bitcast(f32), ALU.subtract).then_inc(w_lo, 1)

                eng.sem_inc(w_lo, 2)
                run_slots(eng, slot, own, LINKS)

                eng.wait_ge(placed, GROUPS)
                own.mark(V.tensor_scalar(pads[:], base[:], pidx[:], None, ALU.add))
                own.wait()
                eng.sem_inc(pad_at, 1)
                for i in range(4):
                    eng.wait_ge(x2_stored[i], GROUPS // 4 * 16)
                kf = tile_no
                ge = flat[:, 256:256 + TILES * E].rearrange("p (k e) -> p k e", e=E)
                rk = flat[:, 1536:1536 + TILES]
                cnt, nf, cum, zero, step = (flat[:, 2048 + 8 * i:2056 + 8 * i] for i in range(5))
                ti = flat[:, 2200:2208].bitcast(i32)
                eng.wait_ge(tabled, 1)
                own.mark(V.memset(zero, 0.0))
                own.mark(V.tensor_tensor(cnt, base[0:1], region[0:1], ALU.subtract))
                own.wait()
                own.mark(V.tensor_scalar(ti, cnt, float(P - 1), None, ALU.add))
                own.wait()
                own.mark(V.tensor_scalar(ti, ti, P.bit_length() - 1, None, ALU.arith_shift_right))
                own.wait()
                own.mark(V.tensor_copy(nf, ti))
                own.wait()
                own.mark(V.tensor_tensor_scan(cum, nf, zero, 0.0, ALU.add, ALU.add))
                own.mark(V.tensor_scalar(step, nf, float(-P), float(REGION), ALU.mult, ALU.add))
                own.wait()
                own.mark(V.tensor_tensor(ge, kf.unsqueeze(2).to_broadcast([1, TILES, E]),
                                         cum.unsqueeze(1).to_broadcast([1, TILES, E]), ALU.is_ge))
                own.wait()
                own.mark(V.tensor_reduce(rk, ge, X, ALU.add))
                own.wait()
                own.mark(V.tensor_scalar(table[:, 0], rk, float(E - 1), None, ALU.min))
                own.mark(V.tensor_tensor(ge, ge, step.unsqueeze(1).to_broadcast([1, TILES, E]), ALU.mult))
                own.wait()
                own.mark(V.tensor_reduce(rk, ge, X, ALU.add))
                own.wait()
                own.mark(V.scalar_tensor_tensor(rk, kf, float(P), rk, ALU.mult, ALU.add))
                own.wait()
                own.mark(V.tensor_scalar(table[:, 1], rk, float(DUMMY), None, ALU.min))
                own.wait()

            @block.tensor
            def _(eng):
                T = nc.tensor
                eng.wait_ge(consts, 7)
                eng.wait_ge(wz_lo, 4)
                eng.wait_ge(wz_loaded, 48)
                eng.wait_ge(bz_in_place, 16)
                rank = psum[7][:, 64:64 + G * E].rearrange("p (g e) -> p g e", g=G)
                total = psum[7][:, 128:128 + E]

                def slot(g, b, r, u, j=None):
                    first, second, third, weights = parts(u, j)
                    if third:
                        eng.wait_ge(chose, g - 1)
                        T.matmul(rank, upper[:], chosen[:], start=True, stop=False, skip_group_check=True)
                        for c in range(1, G):
                            T.matmul(rank[:, c:], ones[:], chosen[:, 0:G - c], start=False, stop=c == G - 1,
                                     skip_group_check=True)
                        for c in range(G):
                            last = T.matmul(total, ones[:], chosen[:, c], start=c == 0, stop=c == G - 1,
                                            skip_group_check=True)
                        last.then_inc(ranks, 1)

                    def second_transposes(half):
                        eng.wait_ge(xn2, (g - 1) * G + 2 * half + 2)
                        need(eng, xt2_done, 2 * (g - 1) + half)
                        for c in (2 * half, 2 * half + 1):
                            for k in range(DC):
                                last = T.transpose(psum[6][:, (c % 2 * DC + k) * P:(c % 2 * DC + k + 1) * P],
                                                   rows[:, (u - 1) % 2, c, k * P:(k + 1) * P], ident[:])
                        last.then_inc(t2_done, 1)

                    def route(half):
                        eng.wait_ge(xt2_done, 2 * (g - 1) + half + 1)
                        for c in (2 * half, 2 * half + 1):
                            for k in range(DC):
                                last = T.matmul(psum[7][:, c * E:(c + 1) * E], xt2[:, c % 2, k], router[:, k],
                                                start=k == 0, stop=k == DC - 1)
                        last.then_inc(logits, 1)

                    def product(c):
                        if c % 2 == 0:
                            eng.wait_ge(lo1, 2 * g + c // 2 + 1)
                        zc = psum[c][:, 0:NZ]
                        T.matmul(zc, ones_row[:], bz[:], start=True, stop=False)
                        for k in range(DC):
                            T.matmul(zc, xt_hi[:, c, k], wz[:, 0, k], start=False, stop=False)
                            T.matmul(zc, xt_hi[:, c, k], wz[:, 1, k], start=False, stop=False)
                            last = T.matmul(zc, xt_lo[:, c, k], wz[:, 0, k], start=False, stop=k == DC - 1)
                        if c == G - 1:
                            last.then_inc(z_done, 1)

                    if first:
                        for half in range(2):
                            eng.wait_ge(xn1, g * G + 2 * half + 2)
                            need(eng, lo1, 2 * g - 1 + half)
                            for c in (2 * half, 2 * half + 1):
                                for k in range(DC):
                                    last = T.transpose(psum[4 + half][:, (c % 2 * DC + k) * P:(c % 2 * DC + k + 1) * P],
                                                       xn[:, u % 2, c, k * P:(k + 1) * P], ident[:])
                            last.then_inc(t1_done, 1)
                    if second:
                        second_transposes(0)
                    if first:
                        need(eng, z_free, g)
                        product(0)
                    if second:
                        second_transposes(1)
                    if first:
                        product(1)
                    if second:
                        if third:
                            eng.wait_ge(placed, g - 1)
                        route(0)
                    if first:
                        product(2)
                        product(3)
                    if second:
                        route(1)

                run_slots(eng, slot)

        load_row = [sem(f"tile_loaded{i}") for i in range(2)]
        stage2_in = [sem(f"stage2_in{i}") for i in range(2)]
        w2_hi = sem("w2_hi")
        w2_lo = sem("w2_lo")
        tx_done = sem("tx_done")
        xh_done = sem("xh_done")
        xl_done = sem("xl_done")
        gate_done = sem("gate_done")
        up_done = sem("up_done")
        act_done = sem("act_done")
        h_done = sem("h_done")
        th_done = sem("th_done")
        hh_done = sem("hh_done")
        hl_done = sem("hl_done")
        down_done = sem("down_done")
        y_ready = sem("y_ready")
        ids_kept = sem("ids_kept")
        added = [sem(f"added{i}") for i in range(2)]

        def run_tiles(eng, slot, last):
            for k in range(4):
                slot(k, k, k // 4)
            with eng.Fori(0, TILES // 4 - 2) as j:
                for u in range(4, 8):
                    slot(4 * j + u, u, j + u // 4)
            for k in range(TILES - 4, TILES + last):
                slot(k, k, k // 4)

        def add_count(k, u, j, n):
            q = u % 4 - n
            return 2 * (j + (q // 4)) + q % 4 // 2 + 1

        xbank, hbank, ybank = psum[4], psum[5], psum[6]
        gates = [(z[:, 0], z[:, 1]), (z[:, 2], z[:, 3])]

        with nc.Block() as block:

            @block.sync
            def _(eng):
                late = QUARTERS * EARLY

                for i in range(QUARTERS * (E - EARLY)):
                    if i >= 2:
                        eng.wait_ge(w2_lo, i - 1)
                    eng.dma_start(stage2[:, i % 2], experts_in[late + i]).then_inc(stage2_in[i % 2], 16)

                def slot(k, u, j):
                    if u >= 2:
                        eng.wait_ge(tx_done, k - 1)
                        eng.wait_ge(ids_kept, k - 1)
                    row = eng.value_load(table[0:1, 1, bass.ds(k, 1)], min_val=0, max_val=DUMMY)
                    eng.dma_start(xg[:, u % 2], sorted_rows[bass.ds(row, P), :]).then_inc(load_row[u % 2], 16)

                run_tiles(eng, slot, 0)

            @block.gpsimd
            def _(eng):
                def keep(k, u, j):
                    wait_apart(eng, load_row[u % 2], 16 * (2 * j + u % 4 // 2 + 1))
                    eng.tensor_copy(idw[:, u % 4], xg[:, u % 2, ID:ROW].bitcast(i32)).then_inc(ids_kept, 1)

                def slot(k, u, j):
                    if u >= 3:
                        eng.wait_ge(added[(u - 3) % 2], 16 * add_count(k, u, j, 3))
                    if u + 1 < TILES:
                        keep(k + 1, u + 1, j + (1 if u % 4 == 3 else 0))
                    if u >= 2:
                        wait_apart(eng, y_ready, k - 1)
                        eng.indirect_dma_start(out, bass.IndirectOffsetOnAxis(idw[:, (u - 2) % 4, 0:1].bitcast(u32), 0),
                                               y[:, u % 2], None, compute_op=ALU.add).then_inc(added[u % 2], 16)

                keep(0, 0, 0)
                run_tiles(eng, slot, 2)
                eng.wait_ge(added[1], TILES // 2 * 16)
                eng.wait_ge(added[0], TILES // 2 * 16)

            @block.scalar
            def _(eng):
                A = nc.scalar

                for i in range(QUARTERS * (E - EARLY)):
                    eng.wait_ge(stage2_in[i % 2], 16 * (i // 2 + 1))
                    A.activation(wall[:, 2 * (EARLY + i // QUARTERS), i % QUARTERS * Q:(i % QUARTERS + 1) * Q],
                                 stage2[:, i % 2], ACT.Copy).then_inc(w2_hi, 1)
                eng.wait_ge(w2_lo, QUARTERS * (E - EARLY))

                def high_x(k, u):
                    eng.wait_ge(tx_done, k + 1)
                    if u >= 2:
                        eng.wait_ge(up_done, k - 1)
                    A.activation(xg_t[:, u % 2, 0].rearrange("p c n -> p (c n)"), xbank[:, 0:D], ACT.Copy)\
                        .then_inc(xh_done, 1)

                def slot(k, u, j):
                    if u + 1 < TILES:
                        high_x(k + 1, u + 1)
                    if u < TILES:
                        eng.wait_ge(gate_done, k + 1)
                        need(eng, th_done, k)
                        A.activation(h[:], gates[u % 2][0], ACT.Silu).then_inc(act_done, 1)
                    if 1 <= u <= TILES:
                        eng.wait_ge(th_done, k)
                        need(eng, down_done, k - 1)
                        A.activation(ht[:, 0].rearrange("p c n -> p (c n)"), hbank, ACT.Copy).then_inc(hh_done, 1)
                    if u >= 2:
                        expert = eng.value_load(table[0:1, 0, bass.ds(k - 2, 1)], min_val=0, max_val=E - 1)
                        eng.wait_ge(down_done, k - 1)
                        eng.wait_ge(ids_kept, k - 1)
                        if u >= 4:
                            eng.wait_ge(added[u % 2], 16 * add_count(k, u, j, 4))
                        A.activation(y[:, u % 2], ybank[:, 0:D], ACT.Copy,
                                     scale=idw[:, (u - 2) % 4, bass.ds(expert + 1, 1)].bitcast(f32)).then_inc(y_ready, 1)

                high_x(0, 0)
                run_tiles(eng, slot, 2)

            @block.vector
            def _(eng):
                V = nc.vector

                for i in range(QUARTERS * (E - EARLY)):
                    part = slice(i % QUARTERS * Q, (i % QUARTERS + 1) * Q)
                    e = EARLY + i // QUARTERS
                    eng.wait_ge(w2_hi, i + 1)
                    V.tensor_tensor(wall[:, 2 * e + 1, part], stage2[:, i % 2], wall[:, 2 * e, part].bitcast(f32),
                                    ALU.subtract).then_inc(w2_lo, 1)

                def low_x(k, u):
                    eng.wait_ge(xh_done, k + 1)
                    V.tensor_tensor(xg_t[:, u % 2, 1].rearrange("p c n -> p (c n)"), xbank[:, 0:D],
                                    xg_t[:, u % 2, 0].rearrange("p c n -> p (c n)").bitcast(f32),
                                    ALU.subtract).then_inc(xl_done, 1)

                def slot(k, u, j):
                    if u + 1 < TILES:
                        low_x(k + 1, u + 1)
                    if u < TILES:
                        eng.wait_ge(act_done, k + 1)
                        eng.wait_ge(up_done, k + 1)
                        V.tensor_tensor(h[:], h[:], gates[u % 2][1], ALU.mult).then_inc(h_done, 1)
                    if 1 <= u <= TILES:
                        eng.wait_ge(hh_done, k)
                        V.tensor_tensor(ht[:, 1].rearrange("p c n -> p (c n)"), hbank,
                                        ht[:, 0].rearrange("p c n -> p (c n)").bitcast(f32),
                                        ALU.subtract).then_inc(hl_done, 1)

                low_x(0, 0)
                run_tiles(eng, slot, 1)

            @block.tensor
            def _(eng):
                T = nc.tensor

                def transpose_x(k, u, j):
                    eng.wait_ge(load_row[u % 2], 16 * (2 * j + u % 4 // 2 + 1))
                    need(eng, xl_done, k)
                    for c in range(DC):
                        last = T.transpose(xbank[:, c * P:(c + 1) * P], xg[:, u % 2, c * P:(c + 1) * P], ident[:])
                    last.then_inc(tx_done, 1)

                def slot(k, u, j):
                    if u + 1 < TILES:
                        transpose_x(k + 1, u + 1, j + (1 if u % 4 == 3 else 0))
                    if u < TILES:
                        e = eng.value_load(table[0:1, 0, bass.ds(k, 1)], min_val=0, max_val=E - 1)
                        hi = wall[:, bass.ds(2 * e, 1), :].rearrange("p a n -> p (a n)")
                        lo = wall[:, bass.ds(2 * e + 1, 1), :].rearrange("p a n -> p (a n)")
                        eng.wait_ge(xl_done, k + 1)
                        if u >= 2:
                            eng.wait_ge(h_done, k - 1)
                        for which, done in ((0, gate_done), (1, up_done)):
                            bank = gates[u % 2][which]
                            for c in range(DC):
                                w = slice((which * DC + c) * F, (which * DC + c + 1) * F)
                                T.matmul(bank, xg_t[:, u % 2, 0, c], hi[:, w], start=c == 0, stop=False)
                                T.matmul(bank, xg_t[:, u % 2, 0, c], lo[:, w], start=False, stop=False)
                                last = T.matmul(bank, xg_t[:, u % 2, 1, c], hi[:, w], start=False, stop=c == DC - 1)
                            last.then_inc(done, 1)
                    if 1 <= u <= TILES:
                        eng.wait_ge(h_done, k)
                        need(eng, hl_done, k - 1)
                        for c in range(FC):
                            last = T.transpose(hbank[:, c * P:(c + 1) * P], h[:, c * P:(c + 1) * P], ident[:])
                        last.then_inc(th_done, 1)
                    if u >= 2:
                        e = eng.value_load(table[0:1, 0, bass.ds(k - 2, 1)], min_val=0, max_val=E - 1)
                        hi = wall[:, bass.ds(2 * e, 1), :].rearrange("p a n -> p (a n)")
                        lo = wall[:, bass.ds(2 * e + 1, 1), :].rearrange("p a n -> p (a n)")
                        eng.wait_ge(hl_done, k - 1)
                        need(eng, y_ready, k - 2)
                        for c in range(FC):
                            w = slice(2 * DC * F + c * D, 2 * DC * F + (c + 1) * D)
                            T.matmul(ybank[:, 0:D], ht[:, 0, c], hi[:, w], start=c == 0, stop=False)
                            T.matmul(ybank[:, 0:D], ht[:, 0, c], lo[:, w], start=False, stop=False)
                            last = T.matmul(ybank[:, 0:D], ht[:, 1, c], hi[:, w], start=False, stop=c == FC - 1)
                        last.then_inc(down_done, 1)

                eng.wait_ge(w2_lo, QUARTERS * (E - EARLY))
                transpose_x(0, 0, 0)
                run_tiles(eng, slot, 2)


def kernel(L0_attn_x, L0_attn_W1, L0_attn_b1, L0_attn_W2, L0_attn_b2, L0_attn_W3, L0_attn_b3, L0_attn_A,
           L0_ffn_router_kernel_DE, L0_ffn_kernel_gating_EDF, L0_ffn_kernel_up_EDF, L0_ffn_kernel_down_EFD):
    import numpy as np
    from concourse import bacc
    from concourse.bass_utils import run_bass_kernel_spmd

    def chunks(a, n):
        a = np.asarray(a)
        lead, width = a.shape[:-2], a.shape[-1]
        a = np.moveaxis(a.reshape(*lead, n, P, width), -3, -2)
        return a.reshape(*lead, P, n * width)

    w = np.concatenate([L0_attn_W1, L0_attn_W2, L0_attn_W3], axis=0)
    experts = np.concatenate([chunks(L0_ffn_kernel_gating_EDF, DC), chunks(L0_ffn_kernel_up_EDF, DC),
                              chunks(L0_ffn_kernel_down_EFD, FC)], axis=-1)
    arrays = {
        "x_in": np.asarray(L0_attn_x).reshape(TOKENS, D),
        "wz_in": chunks(w.T, DC),
        "bz_in": np.concatenate([L0_attn_b1, L0_attn_b2, L0_attn_b3])[None, :],
        "router_in": chunks(L0_ffn_router_kernel_DE, DC).reshape(P, DC, E),
        "experts_in": experts.reshape(E, P, QUARTERS, Q).transpose(0, 2, 1, 3).reshape(E * QUARTERS, P, Q),
    }
    arrays = {name: np.ascontiguousarray(a) for name, a in arrays.items()}
    nc = bacc.Bacc("TRN2", target_bir_lowering=False, num_devices=1)
    args = [nc.dram_tensor(name, a.shape, mybir.dt.from_np(a.dtype), kind="ExternalInput").ap()
            for name, a in arrays.items()]
    out = nc.dram_tensor("out", (TOKENS + P, D), mybir.dt.float32, kind="ExternalOutput").ap()
    moe_program(nc, *args, out)
    r = run_bass_kernel_spmd(nc, [arrays], core_ids=[0])
    return r.results[0]["out"][0:TOKENS].reshape(np.asarray(L0_attn_x).shape)
```

```python
import concourse.bass as bass
from concourse import mybir
from contextlib import ExitStack

P = 128
D = 256
DC = D // P
TOKENS = 8 * 1024
COLS = TOKENS // P
G = 4
GROUPS = COLS // G
N = 16
NZ = D + 2 * N
E = 8
F = 512
FC = F // P
EXPERT = 2 * DC * F + FC * D
QUARTERS = 4
Q = EXPERT // QUARTERS
TOP_K = 2
EPS = 1e-5

REGION = TOKENS + P
ID = D
WT = D + 1
ROW = D + 1 + E
TILES = -(-(TOP_K * TOKENS // P + E - 1) // 4) * 4
DUMMY = E * REGION
DUMP = TOKENS

EARLY = 6
LOOP_FROM, LOOP_TO = 3, GROUPS - 1
SLOTS = GROUPS + 2
LINKS = 35


def moe_program(nc, x_in, wz_in, bz_in, router_in, experts_in, out):
    f32, f32r, bf16 = mybir.dt.float32, mybir.dt.float32r, mybir.dt.bfloat16
    i32, u32 = mybir.dt.int32, mybir.dt.uint32
    ALU = mybir.AluOpType
    ACT = mybir.ActivationFunctionType
    X = mybir.AxisListType.X

    sorted_rows = nc.dram_tensor("sorted_rows", (DUMMY + P, ROW), f32, kind="Internal").ap()
    x_cols = x_in.rearrange("(p t) d -> p t d", t=COLS)
    out_cols = out[0:TOKENS, :].rearrange("(p t) d -> p t d", t=COLS)

    at = [-(-nc.sbuf_base // 32) * 32]

    def place(name, shape, dt):
        size = 1
        for s in shape[1:]:
            size *= s
        size *= 2 if dt == bf16 else 4
        t = nc.alloc_sbuf_tensor_at(name, shape, dt, offset=at[0])
        at[0] += -(-size // 32) * 32
        return t

    ident = place("ident", [P, P], f32)
    table = place("table", [1, 2, TILES], i32)
    weights_at = at[0]
    wall = place("wall", [P, 2 * E, EXPERT], f32r)
    moe_at = at[0]

    at[0] = weights_at + 2 * EARLY * EXPERT * 4
    x = place("x", [P, 4, G, D], f32)
    xn = place("xn", [P, 2, G, D], f32)
    xt_hi = place("xt_hi", [P, G, DC, P], f32r)
    xt_lo = place("xt_lo", [P, G, DC, P], f32r)
    sp = place("sp", [P, G, D], f32)
    rows = place("rows", [P, 2, G, ROW], f32)
    xt2 = place("xt2", [P, G // 2, DC, P], f32)
    wz = place("wz", [P, 2, DC, NZ], f32r)
    bz = place("bz", [2, NZ], f32r)
    ones_row = place("ones_row", [2, P], f32r)
    stage = place("stage", [P, 2, Q], f32)
    router = place("router", [P, DC, E], f32)
    upper = place("upper", [P, P], bf16)
    ones = place("ones", [P, P], bf16)
    ids = place("ids", [P, COLS], i32)
    prio = place("prio", [P, E], f32)
    region = place("region", [P, E], f32)
    pidx = place("pidx", [P, 1], f32)
    base = place("base", [P, E], f32)
    stats_x = place("stats_x", [P, G, 6], f32)
    stats_x2 = place("stats_x2", [P, G, 6], f32)
    mv1 = place("mv1", [P, G, 2], f32)
    mv2 = place("mv2", [P, G, 2], f32)
    ln1 = place("ln1", [P, G], f32)
    y1 = place("y1", [P, G], f32)
    ln2 = place("ln2", [P, G], f32)
    y2 = place("y2", [P, G], f32)
    nw = place("nw", [P, 3, G], f32)
    rstd = place("rstd", [P, 2, G], f32)
    shift = place("shift", [P, 2, G], f32)
    cc = place("cc", [P, G, N], f32)
    bc = place("bc", [P, G, N], f32)
    s_bc = place("s_bc", [P, G], f32)
    g4 = place("g4", [P, 10, G], f32)
    g32 = place("g32", [P, 7, G, E], f32)
    chosen = place("chosen", [P, G, E], bf16)
    pos = place("pos", [P, 2, TOP_K, G], u32)
    pads = place("pads", [P, E], u32)
    assert at[0] <= nc.sbuf_usable_end, (at[0], nc.sbuf_usable_end)

    wz_raw = x[:, 3].rearrange("p a b -> p (a b)")[:, 0:DC * NZ]
    bz_raw = sp[0:1, 0:2].rearrange("p a b -> p (a b)")[:, 0:NZ]
    bz_low = sp[0:1, 2:4].rearrange("p a b -> p (a b)")[:, 0:NZ]

    at[0] = moe_at
    stage2_at = at[0]
    xg_t = place("xg_t", [P, 2, 2, DC, P], f32r)
    h = place("h", [P, F], f32)
    ht = place("ht", [P, 2, FC, P], f32r)
    y = place("y", [P, 2, D], f32)
    xg = place("xg", [P, 2, ROW], f32)
    idw = place("idw", [P, 4, 1 + E], i32)
    assert at[0] <= nc.sbuf_usable_end, (at[0], nc.sbuf_usable_end)
    at[0] = stage2_at
    stage2 = place("stage2", [P, 2, Q], f32)

    ctx = ExitStack()
    with ctx:
        def sem(name):
            return ctx.enter_context(nc.semaphore(name))

        z = ctx.enter_context(nc.psum_tensor("z", [P, G, 512], f32))
        psum = [z[:, i] for i in range(G)] + [
            ctx.enter_context(nc.psum_tensor(f"bank{i}", [P, 512], f32))[:] for i in range(G, 8)]
        z_view = z[:, :, 0:NZ]

        consts = sem("consts")
        ident0 = sem("ident0")
        wz_loaded = sem("wz_loaded")
        wz_hi = sem("wz_hi")
        bz_in_place = sem("bz_in_place")
        wz_lo = sem("wz_lo")
        x_loaded = [sem(f"x_loaded{i}") for i in range(4)]
        x2_stored = [sem(f"x2_stored{i}") for i in range(4)]
        stats1 = sem("stats1")
        rs1 = sem("rs1")
        norm1 = sem("norm1")
        norm2 = sem("norm2")
        xn1 = sem("xn1")
        t1_done = sem("t1_done")
        hi1 = sem("hi1")
        lo1 = sem("lo1")
        z_done = sem("z_done")
        z_free = sem("z_free")
        soft = sem("soft")
        y_done = sem("y_done")
        x2_done = sem("x2_done")
        stats2 = sem("stats2")
        rs2 = sem("rs2")
        xn2 = sem("xn2")
        t2_done = sem("t2_done")
        xt2_done = sem("xt2_done")
        logits = sem("logits")
        shifted = sem("shifted")
        exps = sem("exps")
        gap = sem("gap")
        gap_exp = sem("gap_exp")
        chose = sem("chose")
        ranks = sem("ranks")
        placed = sem("placed")
        ids_in = sem("ids_in")
        scattered = [sem(f"scattered{i}") for i in range(2)]
        stage_in = [sem(f"stage_in{i}") for i in range(2)]
        w_hi = sem("w_hi")
        w_lo = sem("w_lo")
        act_own = sem("act_own")
        dve_own = sem("dve_own")
        passed = {nc.gpsimd: sem("pool_passed"), nc.vector: sem("dve_passed")}
        pad_row = sem("pad_row")
        pad_at = sem("pad_at")
        padded = sem("padded")
        tabled = sem("tabled")

        flat = x[0:1, 0:3].rearrange("p a g d -> p (a g d)")
        tile_no = flat[:, 0:TILES]

        class Own:

            def __init__(self, eng, semaphore):
                self.eng, self.sem, self.base, self.n = eng, semaphore, 0, 0

            def mark(self, instruction):
                instruction.then_inc(self.sem, 1)
                self.n += 1
                return self.base + self.n

            def wait(self, count=None):
                self.eng.wait_ge(self.sem, self.base + self.n if count is None else count)

        def run_slots(eng, slot, own=None, per_slot=0):
            for g in range(-1, LOOP_FROM):
                slot(g, g % 4, g // 4, g)
            if own:
                start = own.base + own.n
            with eng.Fori(0, (LOOP_TO - LOOP_FROM) // 4) as j:
                if own:
                    own.base, own.n = start + j * (4 * per_slot), 0
                for u in range(LOOP_FROM, LOOP_FROM + 4):
                    slot(4 * j + u, u % 4, j + u // 4, u, j)
                if own:
                    assert own.n == 4 * per_slot, own.n
            if own:
                own.base, own.n = start + per_slot * (LOOP_TO - LOOP_FROM), 0
            for g in range(LOOP_TO, SLOTS):
                slot(g, g % 4, g // 4, g)

        def parts(u, j):
            return (u + 1 < GROUPS, 0 <= u < GROUPS, 1 <= u <= GROUPS, 2 <= u, j is not None)

        def need(eng, semaphore, value):
            if not isinstance(value, int) or value > 0:
                eng.wait_ge(semaphore, value)

        def wait_apart(eng, semaphore, value):
            eng.wait_ge(semaphore, value)
            eng.sem_inc(passed[eng], 1)

        def before(b, r, n):
            return (b - n) % 4, r - (1 if b < n else 0)

        def quarter(u, j, i):
            k = 2 * (u - LOOP_FROM) + i
            return 2 * j + k // QUARTERS, k % QUARTERS

        with nc.Block() as block:

            @block.sync
            def _(eng):
                def load_x(g, b):
                    eng.dma_start(x[:, b], x_cols[:, bass.ds(g * G, G), :]).then_inc(x_loaded[b], 16)

                def store_x2(g, b):
                    eng.wait_ge(x2_done, g + 1)
                    eng.dma_start(out_cols[:, bass.ds(g * G, G), :], x[:, b]).then_inc(x2_stored[b], 16)

                load_x(0, 0)
                eng.dma_start(wz_raw, wz_in).then_inc(wz_loaded, 16)
                eng.dma_start(bz_raw, bz_in).then_inc(wz_loaded, 16)
                eng.dma_start(router[:], router_in).then_inc(wz_loaded, 16)
                load_x(1, 1)
                load_x(2, 2)
                eng.wait_ge(wz_lo, 4)
                eng.dma_start(bz[1:2, :].bitcast(f32), bz_low).then_inc(bz_in_place, 16)
                load_x(3, 3)
                with eng.Fori(0, GROUPS // 4 - 1) as j:
                    for u in range(4):
                        g = 4 * j + 4 + u
                        store_x2(4 * j + u, u)
                        eng.wait_ge(xn2, 4 * G * j + G * (u + 1))
                        eng.wait_ge(x2_stored[u], 16 * (j + 1))
                        eng.wait_ge(wz_loaded, 48)
                        load_x(g, u)
                        for i in range(2):
                            k = 8 * j + 2 * u + i
                            eng.wait_ge(w_lo, k + 1)
                            eng.dma_start(stage[:, i], experts_in[bass.ds(k, 1), :, :]
                                          .rearrange("a p n -> p (a n)")).then_inc(stage_in[i], 16)
                for b in range(4):
                    store_x2(GROUPS - 4 + b, b)
                for b in range(4):
                    eng.wait_ge(x2_stored[b], GROUPS // 4 * 16)

            @block.gpsimd
            def _(eng):
                eng.memset(ident[:], 0.0).then_inc(ident0, 1)
                eng.memset(upper[:], 0.0).then_inc(ident0, 1)
                eng.memset(ones[:], 1.0).then_inc(consts, 1)
                eng.iota(ids[:], pattern=[[1, COLS]], base=0, channel_multiplier=COLS).then_inc(consts, 1)
                eng.iota(prio[:], pattern=[[-1, E]], base=E, channel_multiplier=0,
                         allow_small_or_imprecise_dtypes=True).then_inc(consts, 1)
                eng.iota(region[:], pattern=[[REGION, E]], base=0, channel_multiplier=0,
                         allow_small_or_imprecise_dtypes=True).then_inc(consts, 1)
                eng.iota(pidx[:], pattern=[[0, 1]], base=0, channel_multiplier=1,
                         allow_small_or_imprecise_dtypes=True).then_inc(consts, 1)
                eng.wait_ge(consts, 5)
                eng.wait_ge(ident0, 2)
                eng.affine_select(out=ident[:], in_=ident[:], compare_op=ALU.not_equal, fill=1.0, base=0,
                                  pattern=[[-1, P]], channel_multiplier=1).then_inc(consts, 1)
                eng.affine_select(out=upper[:], in_=upper[:], compare_op=ALU.is_ge, fill=1.0, base=0,
                                  pattern=[[-1, P]], channel_multiplier=1).then_inc(consts, 1)

                def slot(g, b, r, u, j=None):
                    enters, first, second, third, weights = parts(u, j)
                    if third:
                        eng.wait_ge(placed, g - 1)
                        wait_apart(eng, ids_in, g - 1)
                        for k in range(TOP_K):
                            for c in range(G):
                                eng.indirect_dma_start(
                                    sorted_rows, bass.IndirectOffsetOnAxis(pos[:, u % 2, k, c:c + 1], 0),
                                    rows[:, u % 2, c, :], None).then_inc(scattered[u % 2], 16)
                                if k == 0 and c == 1 and first:
                                    add_y(g, b)
                    elif first:
                        add_y(g, b)
                    if first:
                        b2, r2 = before(b, r, 2)
                        if u >= 2:
                            wait_apart(eng, scattered[u % 2], 128 * (2 * r2 + b2 // 2 + 1))
                        eng.tensor_copy(rows[:, u % 2, :, ID].bitcast(i32),
                                        ids[:, bass.ds(g * G, G)]).then_inc(ids_in, 1)

                def add_y(g, b):
                    eng.wait_ge(y_done, g + 1)
                    eng.tensor_tensor(x[:, b], x[:, b], sp[:], ALU.add).then_inc(x2_done, 1)

                run_slots(eng, slot)
                for b in range(4):
                    eng.wait_ge(x2_stored[b], GROUPS // 4 * 16)
                eng.iota(tile_no, pattern=[[1, TILES]], base=0, channel_multiplier=0,
                         allow_small_or_imprecise_dtypes=True).then_inc(tabled, 1)
                for i in range(2):
                    eng.wait_ge(scattered[i], GROUPS // 2 * TOP_K * G * 16)
                pad = rows[:, 0, 0, :]
                eng.memset(pad, 0.0).then_inc(pad_row, 1)
                eng.wait_ge(pad_row, 1)
                eng.iota(pad[:, ID:ID + 1].bitcast(i32), pattern=[[0, 1]], base=DUMP,
                         channel_multiplier=1).then_inc(pad_row, 1)
                eng.wait_ge(pad_row, 2)
                eng.wait_ge(pad_at, 1)
                for e in range(E):
                    eng.indirect_dma_start(sorted_rows, bass.IndirectOffsetOnAxis(pads[:, e:e + 1], 0),
                                           pad, None).then_inc(padded, 16)
                eng.dma_start(sorted_rows[DUMMY:DUMMY + P, :], pad).then_inc(padded, 16)
                eng.dma_start(out[DUMP:DUMP + P, :], pad[:, 0:D]).then_inc(padded, 16)
                eng.wait_ge(padded, (E + 2) * 16)

            @block.scalar
            def _(eng):
                own = Own(eng, act_own)
                nc.scalar.preload_act_table_set("natural_log_exp_and_others")
                eng.wait_ge(wz_loaded, 48)
                nc.scalar.activation(wz[:, 0].rearrange("p c n -> p (c n)"), wz_raw, ACT.Copy).then_inc(wz_hi, 1)
                nc.scalar.activation(bz[0:1, :], bz_raw, ACT.Copy).then_inc(wz_hi, 1)
                eng.wait_ge(wz_lo, 4)
                eng.wait_ge(bz_in_place, 16)

                def slot(g, b, r, u, j=None):
                    enters, first, second, third, weights = parts(u, j)
                    b1, r1 = before(b, r, 1)
                    if first:
                        need(eng, z_done, g)
                        for half in range(2):
                            eng.wait_ge(t1_done, 2 * g + half + 1)
                            nc.scalar.activation(xt_hi[:, 2 * half:2 * half + 2].rearrange("p a c n -> p (a c n)"),
                                                 psum[4 + half], ACT.Copy).then_inc(hi1, 1)
                    if third:
                        eng.wait_ge(shifted, g - 1)
                        nc.scalar.activation(g32[:, 1], g32[:, 0], ACT.Exp).then_inc(exps, 1)
                    if weights:
                        for i in range(2):
                            e, q = quarter(u, j, i)
                            eng.wait_ge(stage_in[i], (g - LOOP_FROM + 1) * 16)
                            nc.scalar.activation(wall[:, bass.ds(2 * e, 1), q * Q:(q + 1) * Q]
                                                 .rearrange("p a n -> p (a n)"), stage[:, i], ACT.Copy).then_inc(w_hi, 1)
                    if second:
                        eng.wait_ge(stats2, g)
                        own.mark(nc.scalar.activation(ln2[:], mv2[:, :, 1], ACT.Ln, bias=EPS))
                        own.wait()
                        nc.scalar.activation(y2[:], ln2[:], ACT.Exp, scale=-0.5).then_inc(rs2, 1)
                    if enters:
                        eng.wait_ge(stats1, g + 2)
                        own.mark(nc.scalar.activation(ln1[:], mv1[:, :, 1], ACT.Ln, bias=EPS))
                        own.wait()
                        nc.scalar.activation(y1[:], ln1[:], ACT.Exp, scale=-0.5).then_inc(rs1, 1)
                    if third:
                        eng.wait_ge(gap, g - 1)
                        nc.scalar.activation(g4[:, 6], g4[:, 5], ACT.Exp).then_inc(gap_exp, 1)
                    if second:
                        eng.wait_ge(norm2, g)
                        if u >= 3:
                            b3, r3 = before(b, r, 3)
                            eng.wait_ge(scattered[(u - 3) % 2], 128 * (2 * r3 + b3 // 2 + 1))
                        for c in range(G):
                            nc.scalar.activation(rows[:, (u - 1) % 2, c, 0:D], x[:, b1, c], ACT.Identity,
                                                 bias=shift[:, 1, c:c + 1], scale=rstd[:, 1, c:c + 1]).then_inc(xn2, 1)
                    if first:
                        eng.wait_ge(z_done, g + 1)
                        need(eng, x2_done, g)
                        nc.scalar.activation(cc[:], z_view[:, :, D + N:NZ], ACT.Copy)
                        own.mark(nc.scalar.activation(sp[:], z_view[:, :, 0:D], ACT.Abs))
                        own.wait()
                        own.mark(nc.scalar.activation(sp[:], sp[:], ACT.Exp, scale=-1.0))
                        own.wait()
                        nc.scalar.activation(sp[:], sp[:], ACT.Ln, bias=1.0).then_inc(soft, 1)
                    if enters:
                        eng.wait_ge(norm1, g + 2)
                        for c in range(G):
                            nc.scalar.activation(xn[:, (u + 1) % 2, c], x[:, (b + 1) % 4, c], ACT.Identity,
                                                 bias=shift[:, 0, c:c + 1], scale=rstd[:, 0, c:c + 1]).then_inc(xn1, 1)
                    if second:
                        for half in range(2):
                            eng.wait_ge(t2_done, 2 * g - 1 + half)
                            need(eng, logits, 2 * (g - 1) + half)
                            nc.scalar.activation(xt2[:].rearrange("p a c n -> p (a c n)"),
                                                 psum[6], ACT.Copy).then_inc(xt2_done, 1)

                run_slots(eng, slot, own, 4)

            @block.vector
            def _(eng):
                own = Own(eng, dve_own)
                V = nc.vector
                V.memset(stage[0:2, 0, 0:P], 1.0).then_inc(wz_lo, 1)
                eng.wait_ge(consts, 7)
                eng.wait_ge(wz_lo, 1)
                V.tensor_copy(ones_row[:], stage[0:2, 0, 0:P]).then_inc(wz_lo, 1)
                V.tensor_copy(base[:], region[:]).then_inc(dve_own, 1)
                own.n = 1
                eng.wait_ge(wz_hi, 2)
                V.tensor_tensor(bz_low, bz_raw, bz[0:1, :].bitcast(f32), ALU.subtract).then_inc(wz_lo, 1)
                V.tensor_tensor(wz[:, 1].rearrange("p c n -> p (c n)"), wz_raw,
                                wz[:, 0].rearrange("p c n -> p (c n)").bitcast(f32), ALU.subtract).then_inc(wz_lo, 1)

                def bcast(a):
                    return a.unsqueeze(2).to_broadcast([P, G, E])

                order = prio[:].unsqueeze(1).to_broadcast([P, G, E])
                mx, rec, m1, best1, best2, dlt, edl, w1, w2, tmp4 = (g4[:, i] for i in range(10))
                lsh, ex, pr, t32, oh1, oh2, u32_ = (g32[:, i] for i in range(7))
                lg = psum[7][:, 0:G * E].rearrange("p (g e) -> p g e", g=G)
                rank = psum[7][:, 64:64 + G * E].rearrange("p (g e) -> p g e", g=G)
                total = psum[7][:, 128:128 + E]

                def mark(instruction):
                    return own.mark(instruction)

                def rsqrt_1(mv, y0):
                    return mark(V.tensor_tensor(nw[:, 0], y0[:], y0[:], ALU.mult))

                def rsqrt_2(mv, y0):
                    return mark(V.scalar_tensor_tensor(nw[:, 1], mv[:, :, 1], EPS, nw[:, 0], ALU.add, ALU.mult))

                def rsqrt_3(mv, y0):
                    return mark(V.tensor_scalar(nw[:, 2], nw[:, 1], -0.5, 1.5, ALU.mult, ALU.add))

                def rsqrt_4(mv, y0, n):
                    return mark(V.tensor_tensor(rstd[:, n], y0[:], nw[:, 2], ALU.mult))

                def mean_shift(mv, n):
                    return V.scalar_tensor_tensor(shift[:, n], mv[:, :, 0], -1.0, rstd[:, n], ALU.mult, ALU.mult)

                def slot(g, b, r, u, j=None):
                    enters, first, second, third, weights = parts(u, j)
                    b1, r1 = before(b, r, 1)
                    bn, rn = (b + 1) % 4, (r + 1 if b == 3 else r)
                    if u == -1:
                        bn, rn = 0, 0

                    def weight(i):
                        e, q = quarter(u, j, i)
                        eng.wait_ge(w_hi, 2 * (g - LOOP_FROM) + i + 1)
                        V.tensor_tensor(
                            wall[:, bass.ds(2 * e + 1, 1), q * Q:(q + 1) * Q].rearrange("p a n -> p (a n)"),
                            stage[:, i],
                            wall[:, bass.ds(2 * e, 1), q * Q:(q + 1) * Q].rearrange("p a n -> p (a n)")
                            .bitcast(f32), ALU.subtract).then_inc(w_lo, 1)

                    if third:
                        eng.wait_ge(logits, 2 * (g - 1))
                        route = mark(V.tensor_reduce(mx, lg, X, ALU.max))
                    if first:
                        for half in range(2):
                            eng.wait_ge(hi1, 2 * g + half + 1)
                            V.tensor_tensor(xt_lo[:, 2 * half:2 * half + 2].rearrange("p a c n -> p (a c n)"),
                                            psum[4 + half],
                                            xt_hi[:, 2 * half:2 * half + 2].rearrange("p a c n -> p (a c n)")
                                            .bitcast(f32), ALU.subtract).then_inc(lo1, 1)
                    if third:
                        own.wait(route)
                        V.tensor_tensor(lsh, lg, bcast(mx), ALU.subtract).then_inc(shifted, 1)
                    if second:
                        eng.wait_ge(x2_done, g)
                        for c in range(G):
                            last = V.bn_stats(stats_x2[:, c], x[:, b1, c])
                        measured2 = mark(last)
                    if third:
                        eng.wait_ge(exps, g - 1)
                        route = mark(V.tensor_reduce(tmp4, ex, X, ALU.add))
                    if second:
                        wait_apart(eng, own.sem, measured2)
                        for c in range(G):
                            last = V.bn_aggr(mv2[:, c], stats_x2[:, c])
                        last.then_inc(stats2, 1)
                    if third:
                        own.wait(route)
                        route = mark(V.reciprocal(rec, tmp4))
                    if enters:
                        eng.wait_ge(x_loaded[bn], (rn + 1) * 16)
                        V.bn_stats(stats_x[:, 0], x[:, bn, 0])
                    if third:
                        own.wait(route)
                        route = mark(V.tensor_tensor(pr, ex, bcast(rec), ALU.mult))
                    if enters:
                        V.bn_stats(stats_x[:, 1], x[:, bn, 1])
                    if third:
                        own.wait(route)
                        route = mark(V.tensor_reduce(m1, pr, X, ALU.max))
                    if enters:
                        V.bn_stats(stats_x[:, 2], x[:, bn, 2])
                    if third:
                        own.wait(route)
                        route = mark(V.tensor_tensor(t32, pr, bcast(m1), ALU.is_equal))
                    if enters:
                        measured = mark(V.bn_stats(stats_x[:, 3], x[:, bn, 3]))
                    if third:
                        own.wait(route)
                        route = mark(V.tensor_tensor(t32, t32, order, ALU.mult))
                    if enters:
                        wait_apart(eng, own.sem, measured)
                        for c in range(G):
                            last = V.bn_aggr(mv1[:, c], stats_x[:, c])
                        last.then_inc(stats1, 1)
                    if third:
                        own.wait(route)
                        route = mark(V.tensor_reduce(best1, t32, X, ALU.max))
                    if second:
                        eng.wait_ge(rs2, g)
                        newton = rsqrt_1(mv2, y2)
                    if third:
                        own.wait(route)
                        route = mark(V.tensor_tensor(oh1, t32, bcast(best1), ALU.is_equal))
                    if second:
                        own.wait(newton)
                        newton = rsqrt_2(mv2, y2)
                    if third:
                        own.wait(route)
                        route = mark(V.scalar_tensor_tensor(pr, oh1, -2.0, pr, ALU.mult, ALU.add))
                    if second:
                        own.wait(newton)
                        newton = rsqrt_3(mv2, y2)
                    if third:
                        own.wait(route)
                        route = mark(V.tensor_reduce(tmp4, pr, X, ALU.max))
                    if second:
                        own.wait(newton)
                        newton = rsqrt_4(mv2, y2, 1)
                    if third:
                        own.wait(route)
                        V.tensor_tensor(dlt, tmp4, m1, ALU.subtract).then_inc(gap, 1)
                        route = mark(V.tensor_tensor(t32, pr, bcast(tmp4), ALU.is_equal))
                    if second:
                        own.wait(newton)
                        mean_shift(mv2, 1).then_inc(norm2, 1)
                    if weights:
                        weight(0)
                    if third:
                        own.wait(route)
                        route = mark(V.tensor_tensor(t32, t32, order, ALU.mult))
                    if enters:
                        eng.wait_ge(rs1, g + 2)
                        newton = rsqrt_1(mv1, y1)
                    if third:
                        own.wait(route)
                        route = mark(V.tensor_reduce(best2, t32, X, ALU.max))
                    if enters:
                        own.wait(newton)
                        newton = rsqrt_2(mv1, y1)
                    if third:
                        own.wait(route)
                        route = mark(V.tensor_tensor(oh2, t32, bcast(best2), ALU.is_equal))
                    if enters:
                        own.wait(newton)
                        newton = rsqrt_3(mv1, y1)
                    if third:
                        own.wait(route)
                        V.tensor_tensor(chosen[:], oh1, oh2, ALU.add).then_inc(chose, 1)
                    if enters:
                        own.wait(newton)
                        newton = rsqrt_4(mv1, y1, 0)
                    if third:
                        eng.wait_ge(gap_exp, g - 1)
                        route = mark(V.tensor_scalar(tmp4, edl, 1.0, None, ALU.add))
                    if enters:
                        own.wait(newton)
                        mean_shift(mv1, 0).then_inc(norm1, 1)
                    if third:
                        own.wait(route)
                        route = mark(V.reciprocal(w1, tmp4))
                    if weights:
                        weight(1)
                    if third:
                        own.wait(route)
                        both = mark(V.tensor_tensor(w2, edl, w1, ALU.mult))
                        V.tensor_tensor(t32, oh1, bcast(w1), ALU.mult)
                    if third:
                        own.wait(both)
                        both = mark(V.tensor_tensor(pr, oh2, bcast(w2), ALU.mult))
                        eng.wait_ge(ranks, g - 1)
                        route = mark(V.tensor_tensor(u32_, rank, base[:].unsqueeze(1).to_broadcast([P, G, E]), ALU.add))
                        own.wait(both)
                        both = mark(V.tensor_tensor(rows[:, u % 2, :, WT:WT + E], t32, pr, ALU.add))
                    if first:
                        eng.wait_ge(soft, g + 1)
                        summed = mark(V.tensor_tensor(bc[:], z_view[:, :, D:D + N], cc[:], ALU.mult))
                    if third:
                        own.wait(both)
                        own.wait(route)
                        both = mark(V.tensor_tensor(t32, oh1, u32_, ALU.mult))
                        route = mark(V.tensor_tensor(pr, oh2, u32_, ALU.mult))
                    if first:
                        V.scalar_tensor_tensor(sp[:], z_view[:, :, 0:D], 0.0, sp[:], ALU.max, ALU.add)\
                            .then_inc(z_free, 1)
                        own.wait(summed)
                        summed = mark(V.tensor_reduce(s_bc[:], bc[:], X, ALU.add))
                    if third:
                        own.wait(route)
                        with nc.allow_low_precision(reason="row numbers, exact in float32"):
                            V.tensor_reduce(pos[:, u % 2, 0], t32, X, ALU.add)
                            V.tensor_reduce(pos[:, u % 2, 1], pr, X, ALU.add)
                        V.tensor_tensor(base[:], base[:], total, ALU.add).then_inc(placed, 1)
                    if first:
                        own.wait(summed)
                        eng.wait_ge(z_free, g + 1)
                        for c in range(G):
                            last = V.scalar_tensor_tensor(sp[:, c], xn[:, u % 2, c], s_bc[:, c:c + 1],
                                                          sp[:, c], ALU.mult, ALU.mult)
                        last.then_inc(y_done, 1)

                eng.sem_inc(w_lo, 2)
                run_slots(eng, slot, own, LINKS)

                eng.wait_ge(placed, GROUPS)
                own.mark(V.tensor_scalar(pads[:], base[:], pidx[:], None, ALU.add))
                own.wait()
                eng.sem_inc(pad_at, 1)
                for i in range(4):
                    eng.wait_ge(x2_stored[i], GROUPS // 4 * 16)
                kf = tile_no
                ge = flat[:, 256:256 + TILES * E].rearrange("p (k e) -> p k e", e=E)
                rk = flat[:, 1536:1536 + TILES]
                cnt, nf, cum, zero, step = (flat[:, 2048 + 8 * i:2056 + 8 * i] for i in range(5))
                ti = flat[:, 2200:2208].bitcast(i32)
                eng.wait_ge(tabled, 1)
                own.mark(V.memset(zero, 0.0))
                own.mark(V.tensor_tensor(cnt, base[0:1], region[0:1], ALU.subtract))
                own.wait()
                own.mark(V.tensor_scalar(ti, cnt, float(P - 1), None, ALU.add))
                own.wait()
                own.mark(V.tensor_scalar(ti, ti, P.bit_length() - 1, None, ALU.arith_shift_right))
                own.wait()
                own.mark(V.tensor_copy(nf, ti))
                own.wait()
                own.mark(V.tensor_tensor_scan(cum, nf, zero, 0.0, ALU.add, ALU.add))
                own.mark(V.tensor_scalar(step, nf, float(-P), float(REGION), ALU.mult, ALU.add))
                own.wait()
                own.mark(V.tensor_tensor(ge, kf.unsqueeze(2).to_broadcast([1, TILES, E]),
                                         cum.unsqueeze(1).to_broadcast([1, TILES, E]), ALU.is_ge))
                own.wait()
                own.mark(V.tensor_reduce(rk, ge, X, ALU.add))
                own.wait()
                own.mark(V.tensor_scalar(table[:, 0], rk, float(E - 1), None, ALU.min))
                own.mark(V.tensor_tensor(ge, ge, step.unsqueeze(1).to_broadcast([1, TILES, E]), ALU.mult))
                own.wait()
                own.mark(V.tensor_reduce(rk, ge, X, ALU.add))
                own.wait()
                own.mark(V.scalar_tensor_tensor(rk, kf, float(P), rk, ALU.mult, ALU.add))
                own.wait()
                own.mark(V.tensor_scalar(table[:, 1], rk, float(DUMMY), None, ALU.min))
                own.wait()

            @block.tensor
            def _(eng):
                T = nc.tensor
                eng.wait_ge(consts, 7)
                eng.wait_ge(wz_lo, 4)
                eng.wait_ge(wz_loaded, 48)
                eng.wait_ge(bz_in_place, 16)
                rank = psum[7][:, 64:64 + G * E].rearrange("p (g e) -> p g e", g=G)
                total = psum[7][:, 128:128 + E]

                def slot(g, b, r, u, j=None):
                    enters, first, second, third, weights = parts(u, j)
                    def first_transposes():
                        for half in range(2):
                            eng.wait_ge(xn1, (g + 1) * G + 2 * half + 2)
                            if u >= 0:
                                eng.wait_ge(lo1, 2 * g + 1 + half)
                            for c in (2 * half, 2 * half + 1):
                                for k in range(DC):
                                    last = T.transpose(psum[4 + half][:, (c % 2 * DC + k) * P:(c % 2 * DC + k + 1) * P],
                                                       xn[:, (u + 1) % 2, c, k * P:(k + 1) * P], ident[:])
                            last.then_inc(t1_done, 1)

                    def second_transposes(half):
                        eng.wait_ge(xn2, (g - 1) * G + 2 * half + 2)
                        need(eng, xt2_done, 2 * (g - 1) + half)
                        for c in (2 * half, 2 * half + 1):
                            for k in range(DC):
                                last = T.transpose(psum[6][:, (c % 2 * DC + k) * P:(c % 2 * DC + k + 1) * P],
                                                   rows[:, (u - 1) % 2, c, k * P:(k + 1) * P], ident[:])
                        last.then_inc(t2_done, 1)

                    def route(half):
                        eng.wait_ge(xt2_done, 2 * (g - 1) + half + 1)
                        for c in (2 * half, 2 * half + 1):
                            for k in range(DC):
                                last = T.matmul(psum[7][:, c * E:(c + 1) * E], xt2[:, c % 2, k], router[:, k],
                                                start=k == 0, stop=k == DC - 1)
                        last.then_inc(logits, 1)

                    def product(c):
                        if c % 2 == 0:
                            eng.wait_ge(lo1, 2 * g + c // 2 + 1)
                        zc = psum[c][:, 0:NZ]
                        T.matmul(zc, ones_row[:], bz[:], start=True, stop=False)
                        for k in range(DC):
                            T.matmul(zc, xt_hi[:, c, k], wz[:, 0, k], start=False, stop=False)
                            T.matmul(zc, xt_hi[:, c, k], wz[:, 1, k], start=False, stop=False)
                            last = T.matmul(zc, xt_lo[:, c, k], wz[:, 0, k], start=False, stop=k == DC - 1)
                        if c == G - 1:
                            last.then_inc(z_done, 1)

                    if first:
                        need(eng, z_free, g)
                        for c in range(G):
                            product(c)
                    if third:
                        eng.wait_ge(chose, g - 1)
                        T.matmul(rank, upper[:], chosen[:], start=True, stop=False, skip_group_check=True)
                        for c in range(1, G):
                            T.matmul(rank[:, c:], ones[:], chosen[:, 0:G - c], start=False, stop=c == G - 1,
                                     skip_group_check=True)
                        for c in range(G):
                            last = T.matmul(total, ones[:], chosen[:, c], start=c == 0, stop=c == G - 1,
                                            skip_group_check=True)
                        last.then_inc(ranks, 1)
                    if second:
                        second_transposes(0)
                        if third:
                            eng.wait_ge(placed, g - 1)
                        route(0)
                        second_transposes(1)
                        route(1)
                    if enters:
                        first_transposes()

                run_slots(eng, slot)

        load_row = [sem(f"tile_loaded{i}") for i in range(2)]
        stage2_in = [sem(f"stage2_in{i}") for i in range(2)]
        w2_hi = sem("w2_hi")
        w2_lo = sem("w2_lo")
        tx_done = sem("tx_done")
        xh_done = sem("xh_done")
        xl_done = sem("xl_done")
        gate_done = sem("gate_done")
        up_done = sem("up_done")
        act_done = sem("act_done")
        h_done = sem("h_done")
        th_done = sem("th_done")
        hh_done = sem("hh_done")
        hl_done = sem("hl_done")
        down_done = sem("down_done")
        y_ready = sem("y_ready")
        ids_kept = sem("ids_kept")
        added = [sem(f"added{i}") for i in range(2)]

        def run_tiles(eng, slot, last):
            for k in range(4):
                slot(k, k, k // 4)
            with eng.Fori(0, TILES // 4 - 2) as j:
                for u in range(4, 8):
                    slot(4 * j + u, u, j + u // 4)
            for k in range(TILES - 4, TILES + last):
                slot(k, k, k // 4)

        def add_count(k, u, j, n):
            q = u % 4 - n
            return 2 * (j + (q // 4)) + q % 4 // 2 + 1

        xbank, hbank, ybank = psum[4], psum[5], psum[6]
        gates = [(z[:, 0], z[:, 1]), (z[:, 2], z[:, 3])]

        with nc.Block() as block:

            @block.sync
            def _(eng):
                late = QUARTERS * EARLY

                for i in range(QUARTERS * (E - EARLY)):
                    if i >= 2:
                        eng.wait_ge(w2_lo, i - 1)
                    eng.dma_start(stage2[:, i % 2], experts_in[late + i]).then_inc(stage2_in[i % 2], 16)

                def slot(k, u, j):
                    if u >= 2:
                        eng.wait_ge(tx_done, k - 1)
                        eng.wait_ge(ids_kept, k - 1)
                    row = eng.value_load(table[0:1, 1, bass.ds(k, 1)], min_val=0, max_val=DUMMY)
                    eng.dma_start(xg[:, u % 2], sorted_rows[bass.ds(row, P), :]).then_inc(load_row[u % 2], 16)

                run_tiles(eng, slot, 0)

            @block.gpsimd
            def _(eng):
                def keep(k, u, j):
                    wait_apart(eng, load_row[u % 2], 16 * (2 * j + u % 4 // 2 + 1))
                    eng.tensor_copy(idw[:, u % 4], xg[:, u % 2, ID:ROW].bitcast(i32)).then_inc(ids_kept, 1)

                def slot(k, u, j):
                    if u >= 3:
                        eng.wait_ge(added[(u - 3) % 2], 16 * add_count(k, u, j, 3))
                    if u + 1 < TILES:
                        keep(k + 1, u + 1, j + (1 if u % 4 == 3 else 0))
                    if u >= 2:
                        wait_apart(eng, y_ready, k - 1)
                        eng.indirect_dma_start(out, bass.IndirectOffsetOnAxis(idw[:, (u - 2) % 4, 0:1].bitcast(u32), 0),
                                               y[:, u % 2], None, compute_op=ALU.add).then_inc(added[u % 2], 16)

                keep(0, 0, 0)
                run_tiles(eng, slot, 2)
                eng.wait_ge(added[1], TILES // 2 * 16)
                eng.wait_ge(added[0], TILES // 2 * 16)

            @block.scalar
            def _(eng):
                A = nc.scalar

                for i in range(QUARTERS * (E - EARLY)):
                    eng.wait_ge(stage2_in[i % 2], 16 * (i // 2 + 1))
                    A.activation(wall[:, 2 * (EARLY + i // QUARTERS), i % QUARTERS * Q:(i % QUARTERS + 1) * Q],
                                 stage2[:, i % 2], ACT.Copy).then_inc(w2_hi, 1)
                eng.wait_ge(w2_lo, QUARTERS * (E - EARLY))

                def high_x(k, u):
                    eng.wait_ge(tx_done, k + 1)
                    if u >= 2:
                        eng.wait_ge(up_done, k - 1)
                    A.activation(xg_t[:, u % 2, 0].rearrange("p c n -> p (c n)"), xbank[:, 0:D], ACT.Copy)\
                        .then_inc(xh_done, 1)

                def slot(k, u, j):
                    if u + 1 < TILES:
                        high_x(k + 1, u + 1)
                    if u < TILES:
                        eng.wait_ge(gate_done, k + 1)
                        need(eng, th_done, k)
                        A.activation(h[:], gates[u % 2][0], ACT.Silu).then_inc(act_done, 1)
                    if 1 <= u <= TILES:
                        eng.wait_ge(th_done, k)
                        need(eng, down_done, k - 1)
                        A.activation(ht[:, 0].rearrange("p c n -> p (c n)"), hbank, ACT.Copy).then_inc(hh_done, 1)
                    if u >= 2:
                        expert = eng.value_load(table[0:1, 0, bass.ds(k - 2, 1)], min_val=0, max_val=E - 1)
                        eng.wait_ge(down_done, k - 1)
                        eng.wait_ge(ids_kept, k - 1)
                        if u >= 4:
                            eng.wait_ge(added[u % 2], 16 * add_count(k, u, j, 4))
                        A.activation(y[:, u % 2], ybank[:, 0:D], ACT.Copy,
                                     scale=idw[:, (u - 2) % 4, bass.ds(expert + 1, 1)].bitcast(f32)).then_inc(y_ready, 1)

                high_x(0, 0)
                run_tiles(eng, slot, 2)

            @block.vector
            def _(eng):
                V = nc.vector

                for i in range(QUARTERS * (E - EARLY)):
                    part = slice(i % QUARTERS * Q, (i % QUARTERS + 1) * Q)
                    e = EARLY + i // QUARTERS
                    eng.wait_ge(w2_hi, i + 1)
                    V.tensor_tensor(wall[:, 2 * e + 1, part], stage2[:, i % 2], wall[:, 2 * e, part].bitcast(f32),
                                    ALU.subtract).then_inc(w2_lo, 1)

                def low_x(k, u):
                    eng.wait_ge(xh_done, k + 1)
                    V.tensor_tensor(xg_t[:, u % 2, 1].rearrange("p c n -> p (c n)"), xbank[:, 0:D],
                                    xg_t[:, u % 2, 0].rearrange("p c n -> p (c n)").bitcast(f32),
                                    ALU.subtract).then_inc(xl_done, 1)

                def slot(k, u, j):
                    if u + 1 < TILES:
                        low_x(k + 1, u + 1)
                    if u < TILES:
                        eng.wait_ge(act_done, k + 1)
                        eng.wait_ge(up_done, k + 1)
                        V.tensor_tensor(h[:], h[:], gates[u % 2][1], ALU.mult).then_inc(h_done, 1)
                    if 1 <= u <= TILES:
                        eng.wait_ge(hh_done, k)
                        V.tensor_tensor(ht[:, 1].rearrange("p c n -> p (c n)"), hbank,
                                        ht[:, 0].rearrange("p c n -> p (c n)").bitcast(f32),
                                        ALU.subtract).then_inc(hl_done, 1)

                low_x(0, 0)
                run_tiles(eng, slot, 1)

            @block.tensor
            def _(eng):
                T = nc.tensor

                def transpose_x(k, u, j):
                    eng.wait_ge(load_row[u % 2], 16 * (2 * j + u % 4 // 2 + 1))
                    need(eng, xl_done, k)
                    for c in range(DC):
                        last = T.transpose(xbank[:, c * P:(c + 1) * P], xg[:, u % 2, c * P:(c + 1) * P], ident[:])
                    last.then_inc(tx_done, 1)

                def slot(k, u, j):
                    if u + 1 < TILES:
                        transpose_x(k + 1, u + 1, j + (1 if u % 4 == 3 else 0))
                    if u < TILES:
                        e = eng.value_load(table[0:1, 0, bass.ds(k, 1)], min_val=0, max_val=E - 1)
                        hi = wall[:, bass.ds(2 * e, 1), :].rearrange("p a n -> p (a n)")
                        lo = wall[:, bass.ds(2 * e + 1, 1), :].rearrange("p a n -> p (a n)")
                        eng.wait_ge(xl_done, k + 1)
                        if u >= 2:
                            eng.wait_ge(h_done, k - 1)
                        for which, done in ((0, gate_done), (1, up_done)):
                            bank = gates[u % 2][which]
                            for c in range(DC):
                                w = slice((which * DC + c) * F, (which * DC + c + 1) * F)
                                T.matmul(bank, xg_t[:, u % 2, 0, c], hi[:, w], start=c == 0, stop=False)
                                T.matmul(bank, xg_t[:, u % 2, 0, c], lo[:, w], start=False, stop=False)
                                last = T.matmul(bank, xg_t[:, u % 2, 1, c], hi[:, w], start=False, stop=c == DC - 1)
                            last.then_inc(done, 1)
                    if 1 <= u <= TILES:
                        eng.wait_ge(h_done, k)
                        need(eng, hl_done, k - 1)
                        for c in range(FC):
                            last = T.transpose(hbank[:, c * P:(c + 1) * P], h[:, c * P:(c + 1) * P], ident[:])
                        last.then_inc(th_done, 1)
                    if u >= 2:
                        e = eng.value_load(table[0:1, 0, bass.ds(k - 2, 1)], min_val=0, max_val=E - 1)
                        hi = wall[:, bass.ds(2 * e, 1), :].rearrange("p a n -> p (a n)")
                        lo = wall[:, bass.ds(2 * e + 1, 1), :].rearrange("p a n -> p (a n)")
                        eng.wait_ge(hl_done, k - 1)
                        need(eng, y_ready, k - 2)
                        for c in range(FC):
                            w = slice(2 * DC * F + c * D, 2 * DC * F + (c + 1) * D)
                            T.matmul(ybank[:, 0:D], ht[:, 0, c], hi[:, w], start=c == 0, stop=False)
                            T.matmul(ybank[:, 0:D], ht[:, 0, c], lo[:, w], start=False, stop=False)
                            last = T.matmul(ybank[:, 0:D], ht[:, 1, c], hi[:, w], start=False, stop=c == FC - 1)
                        last.then_inc(down_done, 1)

                eng.wait_ge(w2_lo, QUARTERS * (E - EARLY))
                transpose_x(0, 0, 0)
                run_tiles(eng, slot, 2)


def kernel(L0_attn_x, L0_attn_W1, L0_attn_b1, L0_attn_W2, L0_attn_b2, L0_attn_W3, L0_attn_b3, L0_attn_A,
           L0_ffn_router_kernel_DE, L0_ffn_kernel_gating_EDF, L0_ffn_kernel_up_EDF, L0_ffn_kernel_down_EFD):
    import numpy as np
    from concourse import bacc
    from concourse.bass_utils import run_bass_kernel_spmd

    def chunks(a, n):
        a = np.asarray(a)
        lead, width = a.shape[:-2], a.shape[-1]
        a = np.moveaxis(a.reshape(*lead, n, P, width), -3, -2)
        return a.reshape(*lead, P, n * width)

    w = np.concatenate([L0_attn_W1, L0_attn_W2, L0_attn_W3], axis=0)
    experts = np.concatenate([chunks(L0_ffn_kernel_gating_EDF, DC), chunks(L0_ffn_kernel_up_EDF, DC),
                              chunks(L0_ffn_kernel_down_EFD, FC)], axis=-1)
    arrays = {
        "x_in": np.asarray(L0_attn_x).reshape(TOKENS, D),
        "wz_in": chunks(w.T, DC),
        "bz_in": np.concatenate([L0_attn_b1, L0_attn_b2, L0_attn_b3])[None, :],
        "router_in": chunks(L0_ffn_router_kernel_DE, DC).reshape(P, DC, E),
        "experts_in": experts.reshape(E, P, QUARTERS, Q).transpose(0, 2, 1, 3).reshape(E * QUARTERS, P, Q),
    }
    arrays = {name: np.ascontiguousarray(a) for name, a in arrays.items()}
    nc = bacc.Bacc("TRN2", target_bir_lowering=False, num_devices=1)
    args = [nc.dram_tensor(name, a.shape, mybir.dt.from_np(a.dtype), kind="ExternalInput").ap()
            for name, a in arrays.items()]
    out = nc.dram_tensor("out", (TOKENS + P, D), mybir.dt.float32, kind="ExternalOutput").ap()
    moe_program(nc, *args, out)
    r = run_bass_kernel_spmd(nc, [arrays], core_ids=[0])
    return r.results[0]["out"][0:TOKENS].reshape(np.asarray(L0_attn_x).shape)
```

```python
import concourse.bass as bass
from concourse import mybir
from contextlib import ExitStack

P = 128
D = 256
DC = D // P
TOKENS = 8 * 1024
COLS = TOKENS // P
G = 4
GROUPS = COLS // G
N = 16
NZ = D + 2 * N
E = 8
F = 512
FC = F // P
WIDTHS = 2 * DC * F, FC * D
PIECES = 4
TOP_K = 2
EPS = 1e-5

REGION = TOKENS + P
ID = D
WT = D + 1
ROW = D + 1 + E
TILES = TOP_K * TOKENS // P + E - 1
DUMMY = E * REGION
DUMP = TOKENS

EARLY = 6
LOOP_FROM, LOOP_TO = 3, GROUPS - 1
SLOTS = GROUPS + 2
LINKS = 34


def moe_program(nc, x_in, wz_in, bz_in, router_in, gate_up_in, down_in, out):
    f32, f32r, bf16 = mybir.dt.float32, mybir.dt.float32r, mybir.dt.bfloat16
    i32, u32 = mybir.dt.int32, mybir.dt.uint32
    ALU = mybir.AluOpType
    ACT = mybir.ActivationFunctionType
    X = mybir.AxisListType.X

    sorted_rows = nc.dram_tensor("sorted_rows", (DUMMY + P, ROW), f32, kind="Internal").ap()
    experts_in = gate_up_in, down_in
    x_cols = x_in.rearrange("(p t) d -> p t d", t=COLS)
    out_cols = out[0:TOKENS, :].rearrange("(p t) d -> p t d", t=COLS)

    at = [-(-nc.sbuf_base // 32) * 32]

    def place(name, shape, dt):
        size = 1
        for s in shape[1:]:
            size *= s
        size *= 2 if dt == bf16 else 4
        t = nc.alloc_sbuf_tensor_at(name, shape, dt, offset=at[0])
        at[0] += -(-size // 32) * 32
        return t

    ident = place("ident", [P, P], f32)
    tables = place("tables", [E, 2, TILES], i32)
    table = tables[0:1]
    high, low, raw, late = [], [], [], []
    for name, width in zip(("gate_up", "down"), WIDTHS):
        for part, kept in (("hi", high), ("lo", low)):
            late.append(at[0] + EARLY * width * 4)
            kept.append(place(f"{name}_{part}", [P, E, width], f32r))
        raw_end = at[0]
        at[0] -= E * width * 4
        raw.append(place(f"{name}_raw", [P, E, width], f32))
        assert at[0] == raw_end
    moe_at = at[0]

    def piece(tensors, e, half, i):
        width = WIDTHS[i] // 2
        part = tensors[i][:, bass.ds(e, 1) if not isinstance(e, int) else slice(e, e + 1),
                          half * width:(half + 1) * width]
        return part.rearrange("p a n -> p (a n)")

    at[0] = late[0]
    x = place("x", [P, 4, G, D], f32)
    assert at[0] <= late[0] + (E - EARLY) * WIDTHS[0] * 4
    at[0] = late[1]
    xn = place("xn", [P, 2, G, D], f32)
    sp = place("sp", [P, G, D], f32)
    xt_hi = place("xt_hi", [P, G, DC, P], f32r)
    assert at[0] <= late[1] + (E - EARLY) * WIDTHS[0] * 4
    at[0] = late[2]
    xt_lo = place("xt_lo", [P, G, DC, P], f32r)
    xt2 = place("xt2", [P, G // 2, DC, P], f32)
    assert at[0] <= late[2] + (E - EARLY) * WIDTHS[1] * 4
    at[0] = late[3]
    wz = place("wz", [P, 2, DC, NZ], f32r)
    bz = place("bz", [2, NZ], f32r)
    ones_row = place("ones_row", [2, P], f32r)
    router = place("router", [P, DC, E], f32)
    at[0] = max(at[0], moe_at)
    rows = place("rows", [P, 2, G, ROW], f32)
    pad = place("pad", [P, ROW], f32)
    upper = place("upper", [P, P], bf16)
    ones = place("ones", [P, P], bf16)
    ones_f = place("ones_f", [P, 1], f32)
    ids = place("ids", [P, COLS], i32)
    prio = place("prio", [P, E], f32)
    region = place("region", [P, E], f32)
    base = place("base", [P, E], f32)
    stats_x = place("stats_x", [P, G, 6], f32)
    stats_x2 = place("stats_x2", [P, G, 6], f32)
    mv1 = place("mv1", [P, G, 2], f32)
    mv2 = place("mv2", [P, G, 2], f32)
    ln1 = place("ln1", [P, G], f32)
    y1 = place("y1", [P, G], f32)
    ln2 = place("ln2", [P, G], f32)
    y2 = place("y2", [P, G], f32)
    nw = place("nw", [P, 2, 3, G], f32)
    rstd = place("rstd", [P, 2, G], f32)
    shift = place("shift", [P, 2, G], f32)
    cc = place("cc", [P, G, N], f32)
    bc = place("bc", [P, G, N], f32)
    s_bc = place("s_bc", [P, G], f32)
    g4 = place("g4", [P, 10, G], f32)
    g32 = place("g32", [P, 7, G, E], f32)
    chosen = place("chosen", [P, G, E], bf16)
    pos = place("pos", [P, 2, TOP_K, G], u32)
    ends = place("ends", [1, E], i32)
    tiny = g32[:, 0:2].rearrange("p a g e -> p (a g) e")
    assert at[0] <= nc.sbuf_usable_end, (at[0], nc.sbuf_usable_end)

    wz_raw = x[:, 3].rearrange("p a b -> p (a b)")[:, 0:DC * NZ]
    bz_raw = sp[0:1, 0:2].rearrange("p a b -> p (a b)")[:, 0:NZ]
    bz_low = sp[0:1, 2:4].rearrange("p a b -> p (a b)")[:, 0:NZ]

    at[0] = moe_at
    xg_t = place("xg_t", [P, 2, 2, DC, P], f32r)
    h = place("h", [P, F], f32)
    ht = place("ht", [P, 2, FC, P], f32r)
    y = place("y", [P, 2, D], f32)
    xg = place("xg", [P, 2, ROW], f32)
    idw = place("idw", [P, 4, 1 + E], i32)
    assert at[0] <= nc.sbuf_usable_end, (at[0], nc.sbuf_usable_end)

    ctx = ExitStack()
    with ctx:
        def sem(name):
            return ctx.enter_context(nc.semaphore(name))

        z = ctx.enter_context(nc.psum_tensor("z", [P, G, 512], f32))
        psum = [z[:, i] for i in range(G)] + [
            ctx.enter_context(nc.psum_tensor(f"bank{i}", [P, 512], f32))[:] for i in range(G, 8)]
        z_view = z[:, :, 0:NZ]

        consts = sem("consts")
        ident0 = sem("ident0")
        wz_loaded = sem("wz_loaded")
        wz_hi = sem("wz_hi")
        bz_loaded = sem("bz_loaded")
        bz_split = sem("bz_split")
        bz_in_place = sem("bz_in_place")
        wz_lo = sem("wz_lo")
        x_loaded = [sem(f"x_loaded{i}") for i in range(4)]
        x2_stored = [sem(f"x2_stored{i}") for i in range(4)]
        stats1 = sem("stats1")
        rs1 = sem("rs1")
        norm1 = sem("norm1")
        norm2 = sem("norm2")
        xn1 = sem("xn1")
        t1_done = sem("t1_done")
        hi1 = sem("hi1")
        lo1 = sem("lo1")
        z_done = sem("z_done")
        z_free = sem("z_free")
        c_copied = sem("c_copied")
        soft = sem("soft")
        y_done = sem("y_done")
        x2_done = sem("x2_done")
        stats2 = sem("stats2")
        rs2 = sem("rs2")
        xn2 = sem("xn2")
        t2_done = sem("t2_done")
        xt2_done = sem("xt2_done")
        logits = sem("logits")
        shifted = sem("shifted")
        exps = sem("exps")
        gap = sem("gap")
        gap_exp = sem("gap_exp")
        chose = sem("chose")
        ranks = sem("ranks")
        counted = sem("counted")
        placed = sem("placed")
        ids_in = sem("ids_in")
        scattered = [sem(f"scattered{i}") for i in range(2)]
        raw_in = [[sem(f"raw_in{i}{k}") for k in range(2)] for i in range(2)]
        late_in = [sem(f"late_in{i}") for i in range(E - EARLY)]
        w_hi = sem("w_hi")
        w_lo = sem("w_lo")
        act_own = sem("act_own")
        dve_own = sem("dve_own")
        passed = {nc.gpsimd: sem("pool_passed"), nc.vector: sem("dve_passed")}
        pad_row = sem("pad_row")
        ended = sem("ended")
        padded = sem("padded")
        tile_nos = sem("tile_nos")
        ge_ready = sem("ge_ready")
        tile_sums = sem("tile_sums")

        class Own:

            def __init__(self, eng, semaphore):
                self.eng, self.sem, self.base, self.n = eng, semaphore, 0, 0

            def mark(self, instruction):
                instruction.then_inc(self.sem, 1)
                self.n += 1
                return self.base + self.n

            def wait(self, count=None):
                self.eng.wait_ge(self.sem, self.base + self.n if count is None else count)

        def run_slots(eng, slot, own=None, per_slot=0, setup=None):
            for g in range(-1, LOOP_FROM):
                slot(g, g % 4, g // 4, g)
                if g < 0 and setup:
                    setup()
            if own:
                start = own.base + own.n
            with eng.Fori(0, (LOOP_TO - LOOP_FROM) // 4) as j:
                if own:
                    own.base, own.n = start + j * (4 * per_slot), 0
                for u in range(LOOP_FROM, LOOP_FROM + 4):
                    slot(4 * j + u, u % 4, j + u // 4, u, j)
                if own:
                    assert own.n == 4 * per_slot, own.n
            if own:
                own.base, own.n = start + per_slot * (LOOP_TO - LOOP_FROM), 0
            for g in range(LOOP_TO, SLOTS):
                slot(g, g % 4, g // 4, g)

        def parts(u, j):
            return (u + 1 < GROUPS, 0 <= u < GROUPS, 1 <= u <= GROUPS, 2 <= u, j is not None)

        def need(eng, semaphore, value):
            if not isinstance(value, int) or value > 0:
                eng.wait_ge(semaphore, value)

        def wait_apart(eng, semaphore, value):
            eng.wait_ge(semaphore, value)
            eng.sem_inc(passed[eng], 1)

        def before(b, r, n):
            return (b - n) % 4, r - (1 if b < n else 0)

        def split_now(u, j):
            return 2 * j + (u - LOOP_FROM) // 2, (u - LOOP_FROM) % 2

        with nc.Block() as block:

            @block.sync
            def _(eng):
                def load_x(g, b):
                    eng.dma_start(x[:, b], x_cols[:, bass.ds(g * G, G), :]).then_inc(x_loaded[b], 16)

                def store_x2(g, b):
                    eng.wait_ge(x2_done, g + 1)
                    eng.dma_start(out_cols[:, bass.ds(g * G, G), :], x[:, b]).then_inc(x2_stored[b], 16)

                def load_late(e):
                    for i in range(2):
                        eng.dma_start(raw[i][:, e], experts_in[i][e]).then_inc(late_in[e - EARLY], 16)

                load_x(0, 0)
                eng.dma_start(bz_raw, bz_in).then_inc(bz_loaded, 16)
                eng.dma_start(wz_raw, wz_in).then_inc(wz_loaded, 16)
                eng.dma_start(router[:], router_in).then_inc(wz_loaded, 16)
                load_x(1, 1)
                load_x(2, 2)
                eng.wait_ge(bz_split, 2)
                eng.dma_start(bz[1:2, :].bitcast(f32), bz_low).then_inc(bz_in_place, 16)
                eng.wait_ge(wz_lo, 3)
                load_x(3, 3)
                eng.wait_ge(pad_row, 2)
                eng.dma_start(sorted_rows[DUMMY:DUMMY + P, :], pad[:]).then_inc(padded, 16)
                eng.dma_start(out[DUMP:DUMP + P, :], pad[:, 0:D]).then_inc(padded, 16)
                with eng.Fori(0, GROUPS // 4 - 1) as j:
                    for u in range(4):
                        g = 4 * j + 4 + u
                        store_x2(4 * j + u, u)
                        eng.wait_ge(xn2, 4 * G * j + G * (u + 1))
                        eng.wait_ge(x2_stored[u], 16 * (j + 1))
                        eng.wait_ge(wz_loaded, 32)
                        load_x(g, u)
                        for i in range(2):
                            width = WIDTHS[i] // 2
                            eng.wait_ge(w_hi, 8 * j + 2 * u + i + 1)
                            eng.dma_start(piece(raw, 2 * j + u // 2, u % 2, i),
                                          experts_in[i][bass.ds(2 * j + u // 2, 1), :,
                                                        u % 2 * width:(u % 2 + 1) * width]
                                          .rearrange("a p n -> p (a n)")).then_inc(raw_in[u % 2][i], 16)
                for b in range(4):
                    store_x2(GROUPS - 4 + b, b)
                for b in range(4):
                    eng.wait_ge(x2_stored[b], GROUPS // 4 * 16)
                eng.wait_ge(xn2, GROUPS * G)
                load_late(EARLY)
                eng.wait_ge(logits, 2 * GROUPS)
                load_late(EARLY + 1)
                eng.wait_ge(ended, 1)
                for e in range(E):
                    end = eng.value_load(ends[0:1, e:e + 1], min_val=0, max_val=DUMMY)
                    eng.dma_start(sorted_rows[bass.ds(end, P), :], pad[:]).then_inc(padded, 16)
                eng.wait_ge(padded, (E + 2) * 16)

            @block.gpsimd
            def _(eng):
                eng.memset(ident[:], 0.0).then_inc(ident0, 1)
                eng.memset(upper[:], 0.0).then_inc(ident0, 1)
                eng.memset(ones[:], 1.0).then_inc(consts, 1)
                eng.iota(ids[:], pattern=[[1, COLS]], base=0, channel_multiplier=COLS).then_inc(consts, 1)
                eng.iota(prio[:], pattern=[[-1, E]], base=E, channel_multiplier=0,
                         allow_small_or_imprecise_dtypes=True).then_inc(consts, 1)
                eng.iota(region[:], pattern=[[REGION, E]], base=0, channel_multiplier=0,
                         allow_small_or_imprecise_dtypes=True).then_inc(consts, 1)
                eng.memset(ones_f[:], 1.0).then_inc(consts, 1)
                eng.wait_ge(consts, 5)
                eng.wait_ge(ident0, 2)
                eng.affine_select(out=ident[:], in_=ident[:], compare_op=ALU.not_equal, fill=1.0, base=0,
                                  pattern=[[-1, P]], channel_multiplier=1).then_inc(consts, 1)
                eng.affine_select(out=upper[:], in_=upper[:], compare_op=ALU.is_ge, fill=1.0, base=0,
                                  pattern=[[-1, P]], channel_multiplier=1).then_inc(consts, 1)
                eng.memset(pad[:], 0.0).then_inc(pad_row, 1)
                eng.wait_ge(pad_row, 1)
                eng.iota(pad[:, ID:ID + 1].bitcast(i32), pattern=[[0, 1]], base=DUMP,
                         channel_multiplier=1).then_inc(pad_row, 1)
                eng.iota(tables[:, 0].bitcast(f32), pattern=[[1, TILES]], base=0, channel_multiplier=0,
                         allow_small_or_imprecise_dtypes=True).then_inc(tile_nos, 1)

                def slot(g, b, r, u, j=None):
                    enters, first, second, third, weights = parts(u, j)
                    if third:
                        eng.wait_ge(placed, g - 1)
                        wait_apart(eng, ids_in, g - 1)
                        for k in range(TOP_K):
                            for c in range(G):
                                eng.indirect_dma_start(
                                    sorted_rows, bass.IndirectOffsetOnAxis(pos[:, u % 2, k, c:c + 1], 0),
                                    rows[:, u % 2, c, :], None).then_inc(scattered[u % 2], 16)
                                if k == 1 and c == 0 and first:
                                    add_y(g, b)
                    elif first:
                        add_y(g, b)
                    if first:
                        b2, r2 = before(b, r, 2)
                        if u >= 2:
                            wait_apart(eng, scattered[u % 2], 128 * (2 * r2 + b2 // 2 + 1))
                        eng.tensor_copy(rows[:, u % 2, :, ID].bitcast(i32),
                                        ids[:, bass.ds(g * G, G)]).then_inc(ids_in, 1)

                def add_y(g, b):
                    eng.wait_ge(y_done, g + 1)
                    eng.tensor_tensor(x[:, b], x[:, b], sp[:], ALU.add).then_inc(x2_done, 1)

                run_slots(eng, slot)
                for i in range(2):
                    eng.wait_ge(scattered[i], GROUPS // 2 * TOP_K * G * 16)

            @block.scalar
            def _(eng):
                own = Own(eng, act_own)
                nc.scalar.preload_act_table_set("natural_log_exp_and_others")
                eng.wait_ge(bz_loaded, 16)
                nc.scalar.activation(bz[0:1, :], bz_raw, ACT.Copy).then_inc(bz_split, 1)

                def setup():
                    eng.wait_ge(wz_loaded, 32)
                    nc.scalar.activation(wz[:, 0].rearrange("p c n -> p (c n)"), wz_raw, ACT.Copy).then_inc(wz_hi, 1)
                    eng.wait_ge(bz_in_place, 16)

                def slot(g, b, r, u, j=None):
                    enters, first, second, third, weights = parts(u, j)
                    b1 = (b - 1) % 4
                    if first:
                        need(eng, z_done, 2 * g)
                        for half in range(2):
                            eng.wait_ge(t1_done, 2 * g + half + 1)
                            nc.scalar.activation(xt_hi[:, 2 * half:2 * half + 2].rearrange("p a c n -> p (a c n)"),
                                                 psum[4 + half], ACT.Copy).then_inc(hi1, 1)
                    if weights:
                        for i in range(2):
                            e, half = split_now(u, j)
                            eng.wait_ge(raw_in[half][i], (2 * j + (u - LOOP_FROM) // 2 + 1) * 16)
                            nc.scalar.activation(piece(high, e, half, i), piece(raw, e, half, i), ACT.Copy)\
                                .then_inc(w_hi, 1)
                    if third:
                        eng.wait_ge(shifted, g - 1)
                        nc.scalar.activation(g32[:, 1], g32[:, 0], ACT.Exp).then_inc(exps, 1)
                    if enters:
                        eng.wait_ge(stats1, g + 2)
                        own.mark(nc.scalar.activation(ln1[:], mv1[:, :, 1], ACT.Ln, bias=EPS))
                        own.wait()
                        nc.scalar.activation(y1[:], ln1[:], ACT.Exp, scale=-0.5).then_inc(rs1, 1)
                    if second:
                        eng.wait_ge(stats2, g)
                        own.mark(nc.scalar.activation(ln2[:], mv2[:, :, 1], ACT.Ln, bias=EPS))
                        own.wait()
                        nc.scalar.activation(y2[:], ln2[:], ACT.Exp, scale=-0.5).then_inc(rs2, 1)

                    def norm_x(half):
                        if half == 0:
                            eng.wait_ge(norm1, g + 2)
                            if u >= 1:
                                eng.wait_ge(y_done, g)
                        for c in (2 * half, 2 * half + 1):
                            nc.scalar.activation(xn[:, (u + 1) % 2, c], x[:, (b + 1) % 4, c], ACT.Identity,
                                                 bias=shift[:, 0, c:c + 1], scale=rstd[:, 0, c:c + 1]).then_inc(xn1, 1)

                    def norm_x2(half):
                        if half == 0:
                            eng.wait_ge(norm2, g)
                            if u >= 3:
                                b3, r3 = before(b, r, 3)
                                eng.wait_ge(scattered[(u - 3) % 2], 128 * (2 * r3 + b3 // 2 + 1))
                        for c in (2 * half, 2 * half + 1):
                            nc.scalar.activation(rows[:, (u - 1) % 2, c, 0:D], x[:, b1, c], ACT.Identity,
                                                 bias=shift[:, 1, c:c + 1], scale=rstd[:, 1, c:c + 1]).then_inc(xn2, 1)

                    def absolute(half):
                        eng.wait_ge(z_done, 2 * g + half + 1)
                        if half == 0:
                            need(eng, x2_done, g)
                        cols = slice(2 * half, 2 * half + 2)
                        return nc.scalar.activation(sp[:, cols], z_view[:, cols, 0:D], ACT.Abs)

                    def copy_xt2(half):
                        eng.wait_ge(t2_done, 2 * (g - 1) + half + 1)
                        need(eng, logits, 2 * (g - 1) + half)
                        nc.scalar.activation(xt2[:].rearrange("p a c n -> p (a c n)"),
                                             psum[6], ACT.Copy).then_inc(xt2_done, 1)

                    if enters:
                        norm_x(0)
                    if first:
                        absolute(0)
                    if third:
                        eng.wait_ge(gap, g - 1)
                        nc.scalar.activation(g4[:, 6], g4[:, 5], ACT.Exp).then_inc(gap_exp, 1)
                    if second:
                        norm_x2(0)
                    if first:
                        own.mark(absolute(1))
                        nc.scalar.activation(cc[:], z_view[:, :, D + N:NZ], ACT.Copy).then_inc(c_copied, 1)
                    if second:
                        norm_x2(1)
                    if first:
                        own.wait()
                        own.mark(nc.scalar.activation(sp[:], sp[:], ACT.Exp, scale=-1.0))
                        own.wait()
                        nc.scalar.activation(sp[:], sp[:], ACT.Ln, bias=1.0).then_inc(soft, 1)
                    if second:
                        copy_xt2(0)
                    if enters:
                        norm_x(1)
                    if second:
                        copy_xt2(1)

                eng.sem_inc(w_hi, 4)
                run_slots(eng, slot, own, 4, setup)

                for e in range(EARLY, E):
                    eng.wait_ge(late_in[e - EARLY], 32)
                    for half in range(2):
                        for i in range(2):
                            nc.scalar.activation(piece(high, e, half, i), piece(raw, e, half, i), ACT.Copy)\
                                .then_inc(w_hi, 1)

            @block.vector
            def _(eng):
                own = Own(eng, dve_own)
                V = nc.vector
                eng.wait_ge(bz_split, 1)
                V.tensor_tensor(bz_low, bz_raw, bz[0:1, :].bitcast(f32), ALU.subtract).then_inc(bz_split, 1)

                def setup():
                    V.memset(rows[0:2, 0, 0, 0:P], 1.0).then_inc(wz_lo, 1)
                    eng.wait_ge(wz_lo, 1)
                    V.tensor_copy(ones_row[:], rows[0:2, 0, 0, 0:P]).then_inc(wz_lo, 1)
                    eng.wait_ge(consts, 7)
                    own.mark(V.tensor_copy(base[:], region[:]))
                    eng.wait_ge(wz_hi, 1)
                    V.tensor_tensor(wz[:, 1].rearrange("p c n -> p (c n)"), wz_raw,
                                    wz[:, 0].rearrange("p c n -> p (c n)").bitcast(f32), ALU.subtract)\
                        .then_inc(wz_lo, 1)

                def bcast(a):
                    return a.unsqueeze(2).to_broadcast([P, G, E])

                order = prio[:].unsqueeze(1).to_broadcast([P, G, E])
                mx, rec, m1, best1, best2, dlt, edl, w1, w2, tmp4 = (g4[:, i] for i in range(10))
                lsh, ex, pr, t32, oh1, oh2, u32_ = (g32[:, i] for i in range(7))
                lg = psum[7][:, 0:G * E].rearrange("p (g e) -> p g e", g=G)
                rank = psum[7][:, 64:64 + G * E].rearrange("p (g e) -> p g e", g=G)
                total = psum[7][:, 128:128 + E]

                def mark(instruction):
                    return own.mark(instruction)

                def rsqrt_1(mv, y0, n):
                    return mark(V.tensor_tensor(nw[:, n, 0], y0[:], y0[:], ALU.mult))

                def rsqrt_2(mv, y0, n):
                    return mark(V.scalar_tensor_tensor(nw[:, n, 1], mv[:, :, 1], EPS, nw[:, n, 0], ALU.add, ALU.mult))

                def rsqrt_3(mv, y0, n):
                    return mark(V.tensor_scalar(nw[:, n, 2], nw[:, n, 1], -0.5, 1.5, ALU.mult, ALU.add))

                def rsqrt_4(mv, y0, n):
                    return mark(V.tensor_tensor(rstd[:, n], y0[:], nw[:, n, 2], ALU.mult))

                def mean_shift(mv, n):
                    return V.scalar_tensor_tensor(shift[:, n], mv[:, :, 0], -1.0, rstd[:, n], ALU.mult, ALU.mult)

                def lower_weights(e, half, i):
                    V.tensor_tensor(piece(low, e, half, i), piece(raw, e, half, i),
                                    piece(high, e, half, i).bitcast(f32), ALU.subtract).then_inc(w_lo, 1)

                def slot(g, b, r, u, j=None):
                    enters, first, second, third, weights = parts(u, j)
                    b1 = (b - 1) % 4
                    bn, rn = (b + 1) % 4, (r + 1 if b == 3 else r)
                    if u == -1:
                        bn, rn = 0, 0

                    def lower(half):
                        V.tensor_tensor(xt_lo[:, 2 * half:2 * half + 2].rearrange("p a c n -> p (a c n)"),
                                        psum[4 + half],
                                        xt_hi[:, 2 * half:2 * half + 2].rearrange("p a c n -> p (a c n)")
                                        .bitcast(f32), ALU.subtract).then_inc(lo1, 1)

                    def weight(i):
                        e, half = split_now(u, j)
                        eng.wait_ge(w_hi, 2 * (g - LOOP_FROM) + i + 5)
                        lower_weights(e, half, i)

                    if enters:
                        eng.wait_ge(x_loaded[bn], (rn + 1) * 16)
                        for c in range(G):
                            last = V.bn_stats(stats_x[:, c], x[:, bn, c])
                        measured = mark(last)
                    if first:
                        eng.wait_ge(hi1, 2 * g + 1)
                        lower(0)
                    if enters:
                        wait_apart(eng, own.sem, measured)
                        for c in range(G):
                            last = V.bn_aggr(mv1[:, c], stats_x[:, c])
                        last.then_inc(stats1, 1)
                    if first:
                        eng.wait_ge(hi1, 2 * g + 2)
                        lower(1)
                    if third:
                        eng.wait_ge(logits, 2 * (g - 1))
                        route = mark(V.tensor_reduce(mx, lg, X, ALU.max))
                        own.wait(route)
                        V.tensor_tensor(lsh, lg, bcast(mx), ALU.subtract).then_inc(shifted, 1)
                    if second:
                        eng.wait_ge(x2_done, g)
                        for c in range(G):
                            last = V.bn_stats(stats_x2[:, c], x[:, b1, c])
                        measured = mark(last)
                    if third:
                        eng.wait_ge(exps, g - 1)
                        route = mark(V.tensor_reduce(tmp4, ex, X, ALU.add))
                    if enters:
                        eng.wait_ge(rs1, g + 2)
                        newton = rsqrt_1(mv1, y1, 0)
                    if second:
                        wait_apart(eng, own.sem, measured)
                        for c in range(G):
                            last = V.bn_aggr(mv2[:, c], stats_x2[:, c])
                        last.then_inc(stats2, 1)
                    if third:
                        own.wait(route)
                        route = mark(V.reciprocal(rec, tmp4))
                    if enters:
                        own.wait(newton)
                        newton = rsqrt_2(mv1, y1, 0)
                    if third:
                        own.wait(route)
                        route = mark(V.tensor_tensor(pr, ex, bcast(rec), ALU.mult))
                    if enters:
                        own.wait(newton)
                        newton = rsqrt_3(mv1, y1, 0)
                    if third:
                        own.wait(route)
                        route = mark(V.tensor_reduce(m1, pr, X, ALU.max))
                    if enters:
                        own.wait(newton)
                        newton = rsqrt_4(mv1, y1, 0)
                    if third:
                        own.wait(route)
                        route = mark(V.tensor_tensor(t32, pr, bcast(m1), ALU.is_equal))
                    if enters:
                        own.wait(newton)
                        mean_shift(mv1, 0).then_inc(norm1, 1)
                    if third:
                        own.wait(route)
                        route = mark(V.tensor_tensor(t32, t32, order, ALU.mult))
                    if second:
                        eng.wait_ge(rs2, g)
                        newton = rsqrt_1(mv2, y2, 1)
                    if third:
                        own.wait(route)
                        route = mark(V.tensor_reduce(best1, t32, X, ALU.max))
                    if second:
                        own.wait(newton)
                        newton = rsqrt_2(mv2, y2, 1)
                    if third:
                        own.wait(route)
                        route = mark(V.tensor_tensor(oh1, t32, bcast(best1), ALU.is_equal))
                    if second:
                        own.wait(newton)
                        newton = rsqrt_3(mv2, y2, 1)
                    if third:
                        own.wait(route)
                        route = mark(V.scalar_tensor_tensor(pr, oh1, -2.0, pr, ALU.mult, ALU.add))
                    if second:
                        own.wait(newton)
                        newton = rsqrt_4(mv2, y2, 1)
                    if third:
                        own.wait(route)
                        route = mark(V.tensor_reduce(tmp4, pr, X, ALU.max))
                    if second:
                        own.wait(newton)
                        mean_shift(mv2, 1).then_inc(norm2, 1)
                    if third:
                        own.wait(route)
                        V.tensor_tensor(dlt, tmp4, m1, ALU.subtract).then_inc(gap, 1)
                        route = mark(V.tensor_tensor(t32, pr, bcast(tmp4), ALU.is_equal))
                        own.wait(route)
                        route = mark(V.tensor_tensor(t32, t32, order, ALU.mult))
                        own.wait(route)
                        route = mark(V.tensor_reduce(best2, t32, X, ALU.max))
                        own.wait(route)
                        route = mark(V.tensor_tensor(oh2, t32, bcast(best2), ALU.is_equal))
                        own.wait(route)
                        V.tensor_tensor(chosen[:], oh1, oh2, ALU.add).then_inc(chose, 1)
                        eng.wait_ge(gap_exp, g - 1)
                        route = mark(V.tensor_scalar(tmp4, edl, 1.0, None, ALU.add))
                        own.wait(route)
                        route = mark(V.reciprocal(w1, tmp4))
                        eng.wait_ge(ranks, g - 1)
                        counts = mark(V.tensor_tensor(u32_, rank, base[:].unsqueeze(1).to_broadcast([P, G, E]), ALU.add))
                        own.wait(route)
                        both = mark(V.tensor_tensor(w2, edl, w1, ALU.mult))
                        V.tensor_tensor(t32, oh1, bcast(w1), ALU.mult)
                        own.wait(counts)
                        V.tensor_tensor(base[:], base[:], total, ALU.add).then_inc(counted, 1)
                        own.wait(both)
                        both = mark(V.tensor_tensor(pr, oh2, bcast(w2), ALU.mult))
                    if third:
                        own.wait(both)
                        both = mark(V.tensor_tensor(rows[:, u % 2, :, WT:WT + E], t32, pr, ALU.add))
                        own.wait(both)
                        V.tensor_tensor(t32, oh1, u32_, ALU.mult)
                        route = mark(V.tensor_tensor(pr, oh2, u32_, ALU.mult))
                        own.wait(route)
                        with nc.allow_low_precision(reason="row numbers, exact in float32"):
                            V.tensor_reduce(pos[:, u % 2, 0], t32, X, ALU.add)
                            V.tensor_reduce(pos[:, u % 2, 1], pr, X, ALU.add).then_inc(placed, 1)
                    if weights:
                        weight(0)
                    if first:
                        eng.wait_ge(c_copied, g + 1)
                        summed = mark(V.tensor_tensor(bc[:], z_view[:, :, D:D + N], cc[:], ALU.mult))
                    if weights:
                        weight(1)
                    if first:
                        own.wait(summed)
                        summed = mark(V.tensor_reduce(s_bc[:], bc[:], X, ALU.add))
                    if first:
                        eng.wait_ge(soft, g + 1)
                        V.scalar_tensor_tensor(sp[:], z_view[:, :, 0:D], 0.0, sp[:], ALU.max, ALU.add)\
                            .then_inc(z_free, 1)
                        own.wait(summed)
                        eng.wait_ge(z_free, g + 1)
                        for c in range(G):
                            last = V.scalar_tensor_tensor(sp[:, c], xn[:, u % 2, c], s_bc[:, c:c + 1],
                                                          sp[:, c], ALU.mult, ALU.mult)
                        last.then_inc(y_done, 1)

                run_slots(eng, slot, own, LINKS, setup)

                eng.wait_ge(counted, GROUPS)
                cnt, nf, cum, zero, step, tmp = (tiny[:, i] for i in range(6))
                ti = tiny[:, 6].bitcast(i32)
                cum_e, step_e = tiny[:, 7, 0:1], tiny[:, 7, 1:2]
                tile_no = tables[:, 0].bitcast(f32)
                ge = tables[:, 1].bitcast(f32)
                V.tensor_copy(ends[:], base[0:1]).then_inc(ended, 1)
                own.mark(V.memset(zero, 0.0))
                own.mark(V.tensor_tensor(cnt, base[:], region[:], ALU.subtract))
                own.wait()
                own.mark(V.tensor_scalar(ti, cnt, float(P - 1), None, ALU.add))
                own.wait()
                own.mark(V.tensor_scalar(ti, ti, P.bit_length() - 1, None, ALU.arith_shift_right))
                own.wait()
                own.mark(V.tensor_copy(nf, ti))
                own.wait()
                own.mark(V.tensor_tensor_scan(cum, nf, zero, 0.0, ALU.add, ALU.add))
                own.mark(V.tensor_scalar(step, nf, float(-P), float(REGION), ALU.mult, ALU.add))
                own.wait()
                own.mark(V.tensor_tensor(tmp, cum, ident[:, 0:E], ALU.mult))
                own.mark(V.tensor_tensor(cnt, step, ident[:, 0:E], ALU.mult))
                own.wait()
                own.mark(V.tensor_reduce(cum_e, tmp, X, ALU.add))
                V.tensor_reduce(step_e, cnt, X, ALU.add).then_inc(ge_ready, 1)
                own.wait()
                eng.wait_ge(tile_nos, 1)
                V.tensor_scalar(ge, tile_no, cum_e[0:E], None, ALU.is_ge).then_inc(ge_ready, 1)
                eng.wait_ge(tile_sums, 1)
                own.mark(V.scalar_tensor_tensor(ge[0:1], tile_no[0:1], float(P), psum[6][0:1, 256:256 + TILES],
                                                ALU.mult, ALU.add))
                own.wait()
                own.mark(V.tensor_scalar(table[:, 1], ge[0:1], float(DUMMY), None, ALU.min))
                own.mark(V.tensor_scalar(table[:, 0], psum[6][0:1, 0:TILES], float(E - 1), None, ALU.min))
                own.wait()

                for k in range(PIECES * (E - EARLY)):
                    eng.wait_ge(w_hi, 4 + PIECES * EARLY + k + 1)
                    lower_weights(EARLY + k // PIECES, k % PIECES // 2, k % 2)

            @block.tensor
            def _(eng):
                T = nc.tensor
                eng.wait_ge(consts, 7)

                def setup():
                    eng.wait_ge(wz_lo, 3)
                    eng.wait_ge(wz_loaded, 32)
                    eng.wait_ge(bz_in_place, 16)

                rank = psum[7][:, 64:64 + G * E].rearrange("p (g e) -> p g e", g=G)
                total = psum[7][:, 128:128 + E]

                def slot(g, b, r, u, j=None):
                    enters, first, second, third, weights = parts(u, j)
                    def first_transposes(half):
                        eng.wait_ge(xn1, (g + 1) * G + 2 * half + 2)
                        if u >= 0:
                            eng.wait_ge(lo1, 2 * g + 1 + half)
                        for c in (2 * half, 2 * half + 1):
                            for k in range(DC):
                                last = T.transpose(psum[4 + half][:, (c % 2 * DC + k) * P:(c % 2 * DC + k + 1) * P],
                                                   xn[:, (u + 1) % 2, c, k * P:(k + 1) * P], ident[:])
                        last.then_inc(t1_done, 1)

                    def second_transposes(half):
                        eng.wait_ge(xn2, (g - 1) * G + 2 * half + 2)
                        need(eng, xt2_done, 2 * (g - 1) + half)
                        for c in (2 * half, 2 * half + 1):
                            for k in range(DC):
                                last = T.transpose(psum[6][:, (c % 2 * DC + k) * P:(c % 2 * DC + k + 1) * P],
                                                   rows[:, (u - 1) % 2, c, k * P:(k + 1) * P], ident[:])
                        last.then_inc(t2_done, 1)

                    def route(half):
                        eng.wait_ge(xt2_done, 2 * (g - 1) + half + 1)
                        if half == 0 and third:
                            eng.wait_ge(counted, g - 1)
                        for c in (2 * half, 2 * half + 1):
                            for k in range(DC):
                                last = T.matmul(psum[7][:, c * E:(c + 1) * E], xt2[:, c % 2, k], router[:, k],
                                                start=k == 0, stop=k == DC - 1)
                        last.then_inc(logits, 1)

                    def product(c):
                        if c % 2 == 0:
                            eng.wait_ge(lo1, 2 * g + c // 2 + 1)
                        zc = psum[c][:, 0:NZ]
                        T.matmul(zc, ones_row[:], bz[:], start=True, stop=False)
                        for k in range(DC):
                            T.matmul(zc, xt_hi[:, c, k], wz[:, 0, k], start=False, stop=False)
                            T.matmul(zc, xt_hi[:, c, k], wz[:, 1, k], start=False, stop=False)
                            last = T.matmul(zc, xt_lo[:, c, k], wz[:, 0, k], start=False, stop=k == DC - 1)
                        if c % 2 == 1:
                            last.then_inc(z_done, 1)

                    if first:
                        need(eng, z_free, g)
                        for c in range(G):
                            product(c)
                    if third:
                        eng.wait_ge(chose, g - 1)
                        T.matmul(rank, upper[:], chosen[:], start=True, stop=False, skip_group_check=True)
                        for c in range(1, G):
                            T.matmul(rank[:, c:], ones[:], chosen[:, 0:G - c], start=False, stop=c == G - 1,
                                     skip_group_check=True)
                        for c in range(G):
                            last = T.matmul(total, ones[:], chosen[:, c], start=c == 0, stop=c == G - 1,
                                            skip_group_check=True)
                        last.then_inc(ranks, 1)
                    if second:
                        second_transposes(0)
                    if enters:
                        first_transposes(0)
                        if second:
                            route(0)
                    if second:
                        second_transposes(1)
                    if enters:
                        first_transposes(1)
                    elif second:
                        route(0)
                    if second:
                        route(1)

                run_slots(eng, slot, setup=setup)

                eng.wait_ge(ge_ready, 2)
                for i, ones_or_step in enumerate((ones_f[0:E], tiny[0:E, 7, 1:2])):
                    last = T.matmul(psum[6][0:1, 256 * i:256 * i + TILES], ones_or_step,
                                    tables[:, 1].bitcast(f32), start=True, stop=True, skip_group_check=True)
                last.then_inc(tile_sums, 1)

        load_row = [sem(f"tile_loaded{i}") for i in range(2)]
        tx_done = sem("tx_done")
        xh_done = sem("xh_done")
        xl_done = sem("xl_done")
        gate_done = sem("gate_done")
        up_done = sem("up_done")
        act_done = sem("act_done")
        h_done = sem("h_done")
        th_done = sem("th_done")
        hh_done = sem("hh_done")
        hl_done = sem("hl_done")
        down_done = sem("down_done")
        y_ready = sem("y_ready")
        ids_kept = sem("ids_kept")
        added = [sem(f"added{i}") for i in range(2)]

        def run_tiles(eng, slot, last):
            for k in range(4):
                slot(k, k, k // 4)
            loops = TILES // 4 - 2
            with eng.Fori(0, loops) as j:
                for u in range(4, 8):
                    slot(4 * j + u, u, j + u // 4)
            for k in range(4 * (loops + 1), TILES + last):
                slot(k, k, k // 4)

        def add_count(k, u, j, n):
            q = u % 4 - n
            return 2 * (j + (q // 4)) + q % 4 // 2 + 1

        xbank, hbank, ybank = psum[4], psum[5], psum[6]
        gates = [(z[:, 0], z[:, 1]), (z[:, 2], z[:, 3])]

        with nc.Block() as block:

            @block.sync
            def _(eng):
                def slot(k, u, j):
                    if u >= 2:
                        eng.wait_ge(tx_done, k - 1)
                        eng.wait_ge(ids_kept, k - 1)
                    row = eng.value_load(table[0:1, 1, bass.ds(k, 1)], min_val=0, max_val=DUMMY)
                    eng.dma_start(xg[:, u % 2], sorted_rows[bass.ds(row, P), :]).then_inc(load_row[u % 2], 16)

                run_tiles(eng, slot, 0)

            @block.gpsimd
            def _(eng):
                def keep(k, u, j):
                    wait_apart(eng, load_row[u % 2], 16 * (2 * j + u % 4 // 2 + 1))
                    eng.tensor_copy(idw[:, u % 4], xg[:, u % 2, ID:ROW].bitcast(i32)).then_inc(ids_kept, 1)

                def slot(k, u, j):
                    if u >= 3:
                        eng.wait_ge(added[(u - 3) % 2], 16 * add_count(k, u, j, 3))
                    if u + 1 < TILES:
                        keep(k + 1, u + 1, j + (1 if u % 4 == 3 else 0))
                    if u >= 2:
                        wait_apart(eng, y_ready, k - 1)
                        eng.indirect_dma_start(out, bass.IndirectOffsetOnAxis(idw[:, (u - 2) % 4, 0:1].bitcast(u32), 0),
                                               y[:, u % 2], None, compute_op=ALU.add).then_inc(added[u % 2], 16)

                keep(0, 0, 0)
                run_tiles(eng, slot, 2)
                eng.wait_ge(added[0], (TILES + 1) // 2 * 16)
                eng.wait_ge(added[1], TILES // 2 * 16)

            @block.scalar
            def _(eng):
                A = nc.scalar

                def high_x(k, u):
                    eng.wait_ge(tx_done, k + 1)
                    if u >= 2:
                        eng.wait_ge(up_done, k - 1)
                    A.activation(xg_t[:, u % 2, 0].rearrange("p c n -> p (c n)"), xbank[:, 0:D], ACT.Copy)\
                        .then_inc(xh_done, 1)

                def slot(k, u, j):
                    if u + 1 < TILES:
                        high_x(k + 1, u + 1)
                    if u < TILES:
                        eng.wait_ge(gate_done, k + 1)
                        need(eng, th_done, k)
                        A.activation(h[:], gates[u % 2][0], ACT.Silu).then_inc(act_done, 1)
                    if 1 <= u <= TILES:
                        eng.wait_ge(th_done, k)
                        need(eng, down_done, k - 1)
                        A.activation(ht[:, 0].rearrange("p c n -> p (c n)"), hbank, ACT.Copy).then_inc(hh_done, 1)
                    if u >= 2:
                        expert = eng.value_load(table[0:1, 0, bass.ds(k - 2, 1)], min_val=0, max_val=E - 1)
                        eng.wait_ge(down_done, k - 1)
                        eng.wait_ge(ids_kept, k - 1)
                        if u >= 4:
                            eng.wait_ge(added[u % 2], 16 * add_count(k, u, j, 4))
                        A.activation(y[:, u % 2], ybank[:, 0:D], ACT.Copy,
                                     scale=idw[:, (u - 2) % 4, bass.ds(expert + 1, 1)].bitcast(f32)).then_inc(y_ready, 1)

                nc.scalar.preload_act_table_set("silu_and_others")
                high_x(0, 0)
                run_tiles(eng, slot, 2)

            @block.vector
            def _(eng):
                V = nc.vector

                def low_x(k, u):
                    eng.wait_ge(xh_done, k + 1)
                    V.tensor_tensor(xg_t[:, u % 2, 1].rearrange("p c n -> p (c n)"), xbank[:, 0:D],
                                    xg_t[:, u % 2, 0].rearrange("p c n -> p (c n)").bitcast(f32),
                                    ALU.subtract).then_inc(xl_done, 1)

                def slot(k, u, j):
                    if u + 1 < TILES:
                        low_x(k + 1, u + 1)
                    if u < TILES:
                        eng.wait_ge(act_done, k + 1)
                        eng.wait_ge(up_done, k + 1)
                        V.tensor_tensor(h[:], h[:], gates[u % 2][1], ALU.mult).then_inc(h_done, 1)
                    if 1 <= u <= TILES:
                        eng.wait_ge(hh_done, k)
                        V.tensor_tensor(ht[:, 1].rearrange("p c n -> p (c n)"), hbank,
                                        ht[:, 0].rearrange("p c n -> p (c n)").bitcast(f32),
                                        ALU.subtract).then_inc(hl_done, 1)

                low_x(0, 0)
                run_tiles(eng, slot, 1)

            @block.tensor
            def _(eng):
                T = nc.tensor

                def transpose_x(k, u, j):
                    eng.wait_ge(load_row[u % 2], 16 * (2 * j + u % 4 // 2 + 1))
                    need(eng, xl_done, k)
                    for c in range(DC):
                        last = T.transpose(xbank[:, c * P:(c + 1) * P], xg[:, u % 2, c * P:(c + 1) * P], ident[:])
                    last.then_inc(tx_done, 1)

                def slot(k, u, j):
                    if u + 1 < TILES:
                        transpose_x(k + 1, u + 1, j + (1 if u % 4 == 3 else 0))
                    if u < TILES:
                        e = eng.value_load(table[0:1, 0, bass.ds(k, 1)], min_val=0, max_val=E - 1)
                        hi, lo = (t[0][:, bass.ds(e, 1), :].rearrange("p a n -> p (a n)") for t in (high, low))
                        eng.wait_ge(xl_done, k + 1)
                        if u >= 2:
                            eng.wait_ge(h_done, k - 1)
                        for which, done in ((0, gate_done), (1, up_done)):
                            bank = gates[u % 2][which]
                            for c in range(DC):
                                w = slice((which * DC + c) * F, (which * DC + c + 1) * F)
                                T.matmul(bank, xg_t[:, u % 2, 0, c], hi[:, w], start=c == 0, stop=False)
                                T.matmul(bank, xg_t[:, u % 2, 0, c], lo[:, w], start=False, stop=False)
                                last = T.matmul(bank, xg_t[:, u % 2, 1, c], hi[:, w], start=False, stop=c == DC - 1)
                            last.then_inc(done, 1)
                    if 1 <= u <= TILES:
                        eng.wait_ge(h_done, k)
                        need(eng, hl_done, k - 1)
                        for c in range(FC):
                            last = T.transpose(hbank[:, c * P:(c + 1) * P], h[:, c * P:(c + 1) * P], ident[:])
                        last.then_inc(th_done, 1)
                    if u >= 2:
                        e = eng.value_load(table[0:1, 0, bass.ds(k - 2, 1)], min_val=0, max_val=E - 1)
                        hi, lo = (t[1][:, bass.ds(e, 1), :].rearrange("p a n -> p (a n)") for t in (high, low))
                        eng.wait_ge(hl_done, k - 1)
                        need(eng, y_ready, k - 2)
                        for c in range(FC):
                            w = slice(c * D, (c + 1) * D)
                            T.matmul(ybank[:, 0:D], ht[:, 0, c], hi[:, w], start=c == 0, stop=False)
                            T.matmul(ybank[:, 0:D], ht[:, 0, c], lo[:, w], start=False, stop=False)
                            last = T.matmul(ybank[:, 0:D], ht[:, 1, c], hi[:, w], start=False, stop=c == FC - 1)
                        last.then_inc(down_done, 1)

                transpose_x(0, 0, 0)
                run_tiles(eng, slot, 2)


def kernel(L0_attn_x, L0_attn_W1, L0_attn_b1, L0_attn_W2, L0_attn_b2, L0_attn_W3, L0_attn_b3, L0_attn_A,
           L0_ffn_router_kernel_DE, L0_ffn_kernel_gating_EDF, L0_ffn_kernel_up_EDF, L0_ffn_kernel_down_EFD):
    import numpy as np
    from concourse import bacc
    from concourse.bass_utils import run_bass_kernel_spmd

    def chunks(a, n):
        a = np.asarray(a)
        lead, width = a.shape[:-2], a.shape[-1]
        a = np.moveaxis(a.reshape(*lead, n, P, width), -3, -2)
        return a.reshape(*lead, P, n * width)

    w = np.concatenate([L0_attn_W1, L0_attn_W2, L0_attn_W3], axis=0)
    arrays = {
        "x_in": np.asarray(L0_attn_x).reshape(TOKENS, D),
        "wz_in": chunks(w.T, DC),
        "bz_in": np.concatenate([L0_attn_b1, L0_attn_b2, L0_attn_b3])[None, :],
        "router_in": chunks(L0_ffn_router_kernel_DE, DC).reshape(P, DC, E),
        "gate_up_in": np.concatenate([chunks(L0_ffn_kernel_gating_EDF, DC), chunks(L0_ffn_kernel_up_EDF, DC)], axis=-1),
        "down_in": chunks(L0_ffn_kernel_down_EFD, FC),
    }
    arrays = {name: np.ascontiguousarray(a) for name, a in arrays.items()}
    nc = bacc.Bacc("TRN2", target_bir_lowering=False, num_devices=1)
    args = [nc.dram_tensor(name, a.shape, mybir.dt.from_np(a.dtype), kind="ExternalInput").ap()
            for name, a in arrays.items()]
    out = nc.dram_tensor("out", (TOKENS + P, D), mybir.dt.float32, kind="ExternalOutput").ap()
    moe_program(nc, *args, out)
    r = run_bass_kernel_spmd(nc, [arrays], core_ids=[0])
    return r.results[0]["out"][0:TOKENS].reshape(np.asarray(L0_attn_x).shape)
```
